# Optimizing a Trainium2 kernel written in Bass

```python
import numpy as np
import jax
import jax.numpy as jnp

def _softmax(x, axis=-1):
    return jax.nn.softmax(x, axis=axis)

def _gelu(x):
    return jax.nn.gelu(x, approximate=True)

def _silu(x):
    return jax.nn.silu(x)

def _sigmoid(x):
    return jax.nn.sigmoid(x)

def _layernorm(x, axis=-1, eps=1e-05):
    m = jnp.mean(x, axis=axis, keepdims=True)
    v = jnp.var(x, axis=axis, keepdims=True)
    return (x - m) / jnp.sqrt(v + eps)

def _scatter_add(tgt, idx, src, axis=0):
    return tgt.at[idx].add(src)

def _segment_sum(src, seg, n):
    return jax.ops.segment_sum(src, seg, n)
kernel_name = 'mk_decoder_preln_d1_seqx_r4_9330de'

def setup_inputs(seed: int=0):
    np.random.seed(seed)
    _w = jnp.asarray

    def _rec_inputs():
        import jax
        import jax.numpy as jnp
        _rk = jax.random.key(seed)
        x = -0.0003929 + 0.9999 * jax.random.normal(jax.random.fold_in(_rk, 1), (8, 256, 1024), jnp.float32)
        _lenS = 256 - jax.random.randint(jax.random.fold_in(_rk, 7), (8,), 0, max(1, 256 // 4) + 1, jnp.int32)
        _lenS2 = 256 - jax.random.randint(jax.random.fold_in(_rk, 8), (8,), 0, max(1, 256 // 4) + 1, jnp.int32)
        _ctx_4096P = jax.random.normal(jax.random.fold_in(_rk, 11), (8, 16, 1024), jnp.float32)
        _ctx_4096c = jax.random.dirichlet(jax.random.fold_in(_rk, 511), 0.3 * jnp.ones((16,), jnp.float32), (8, 256))
        _ctx_4096t = jnp.einsum('bsk,bkd->bsd', _ctx_4096c, _ctx_4096P)
        _ctx_4096t = _ctx_4096t * jax.lax.rsqrt(jnp.mean(jnp.square(_ctx_4096t)) + 1e-12) * 0.953939
        ctx_4096 = 2.81802e-05 + 1.00001 * (_ctx_4096t + 0.3 * jax.random.normal(jax.random.fold_in(_rk, 611), (8, 256, 1024), jnp.float32))
        return (x, ctx_4096)
    x, ctx_4096 = _rec_inputs()

    def _L0_attn_setup():
        import jax, jax.numpy as jnp
        import numpy as np
        HIDDEN = 1024
        N_HEADS = 32
        N_KV_HEADS = 8
        HEAD_DIM = HIDDEN // N_HEADS
        N_REP = N_HEADS // N_KV_HEADS
        KV_DIM = N_KV_HEADS * HEAD_DIM

        def _kaiming_uniform(key, out_f, in_f):
            bound = 1.0 / np.sqrt(in_f)
            return jax.random.uniform(key, (out_f, in_f), jnp.float32, -bound, bound)

        def bitnet_linear(x, weight, scale_param):
            s = jnp.maximum(jnp.mean(jnp.abs(weight), axis=1), 1e-08)
            binary_w = jnp.sign(weight / s[:, None])
            y = jnp.einsum('bsi,oi->bso', x, binary_w)
            y = y * (s * scale_param)[None, None, :]
            return jnp.nan_to_num(y, nan=0.0, posinf=1000000.0, neginf=-1000000.0)
        key = jax.random.key(seed)
        ks = jax.random.split(key, 5)
        return {'hidden_states': jax.random.normal(ks[0], (1, 512, HIDDEN), jnp.float32), 'q_weight': _kaiming_uniform(ks[1], HIDDEN, HIDDEN), 'q_scale': jnp.ones((HIDDEN,), jnp.float32), 'k_weight': _kaiming_uniform(ks[2], KV_DIM, HIDDEN), 'k_scale': jnp.ones((KV_DIM,), jnp.float32), 'v_weight': _kaiming_uniform(ks[3], KV_DIM, HIDDEN), 'v_scale': jnp.ones((KV_DIM,), jnp.float32), 'o_weight': _kaiming_uniform(ks[4], HIDDEN, HIDDEN), 'o_scale': jnp.ones((HIDDEN,), jnp.float32)}
    _L0_attn_all = _L0_attn_setup()
    _L0_attn_in = {k: v for k, v in _L0_attn_all.items() if k in ('q_weight', 'q_scale', 'k_weight', 'k_scale', 'v_weight', 'v_scale', 'o_weight', 'o_scale')}
    del _L0_attn_all

    def _L0_xattn_setup():
        import jax, jax.numpy as jnp
        import numpy as np
        B, N, NKV = (2, 512, 512)
        E = 1024
        H = 16
        HD = E // H
        LQ = E // 8
        LKV = E // 16
        key = jax.random.key(seed)
        ks = jax.random.split(key, 6)
        Q = jax.random.normal(ks[0], (B, N, E), dtype=jnp.float32)
        K = jax.random.normal(ks[1], (B, NKV, E), dtype=jnp.float32)
        Wq_d = jax.random.normal(ks[2], (E, LQ), dtype=jnp.float32) / np.sqrt(E)
        W_qk = jax.random.normal(ks[3], (LQ, H * LKV), dtype=jnp.float32) / np.sqrt(LQ)
        Wkv_d = jax.random.normal(ks[4], (E, LKV), dtype=jnp.float32) / np.sqrt(E)
        Wv_u = jax.random.normal(ks[5], (LKV, H * HD), dtype=jnp.float32) / np.sqrt(LKV)
        return {'Q': Q, 'K': K, 'Wq_d': Wq_d, 'W_qk': W_qk, 'Wkv_d': Wkv_d, 'Wv_u': Wv_u}
    _L0_xattn_all = _L0_xattn_setup()
    _L0_xattn_in = {k: v for k, v in _L0_xattn_all.items() if k in ('Wq_d', 'W_qk', 'Wkv_d', 'Wv_u')}
    del _L0_xattn_all

    def _L0_ffn_setup():
        import jax, jax.numpy as jnp
        import numpy as np
        HIDDEN = 1024
        INTER = 2752
        RANK = 256
        B, S = (2, 512)
        key = jax.random.key(seed)
        ks = jax.random.split(key, 7)
        sc = 0.02
        return {'x': jax.random.normal(ks[0], (B, S, HIDDEN), dtype=jnp.float32), 'U1': jax.random.normal(ks[1], (HIDDEN, RANK), dtype=jnp.float32) * sc, 'V1': jax.random.normal(ks[2], (RANK, 2 * INTER), dtype=jnp.float32) * sc, 'U2': jax.random.normal(ks[3], (INTER, RANK), dtype=jnp.float32) * sc, 'V2': jax.random.normal(ks[4], (RANK, HIDDEN), dtype=jnp.float32) * sc, 'b1': jax.random.normal(ks[5], (2 * INTER,), dtype=jnp.float32) * sc, 'b2': jax.random.normal(ks[6], (HIDDEN,), dtype=jnp.float32) * sc}
    _L0_ffn_all = _L0_ffn_setup()
    _L0_ffn_in = {k: v for k, v in _L0_ffn_all.items() if k in ('U1', 'V1', 'U2', 'V2', 'b1', 'b2')}
    del _L0_ffn_all
    return {'x': x, 'ctx_4096': ctx_4096, 'L0_attn_q_weight': _L0_attn_in['q_weight'], 'L0_attn_q_scale': _L0_attn_in['q_scale'], 'L0_attn_k_weight': _L0_attn_in['k_weight'], 'L0_attn_k_scale': _L0_attn_in['k_scale'], 'L0_attn_v_weight': _L0_attn_in['v_weight'], 'L0_attn_v_scale': _L0_attn_in['v_scale'], 'L0_attn_o_weight': _L0_attn_in['o_weight'], 'L0_attn_o_scale': _L0_attn_in['o_scale'], 'L0_xattn_Wq_d': _L0_xattn_in['Wq_d'], 'L0_xattn_W_qk': _L0_xattn_in['W_qk'], 'L0_xattn_Wkv_d': _L0_xattn_in['Wkv_d'], 'L0_xattn_Wv_u': _L0_xattn_in['Wv_u'], 'L0_ffn_U1': _L0_ffn_in['U1'], 'L0_ffn_V1': _L0_ffn_in['V1'], 'L0_ffn_U2': _L0_ffn_in['U2'], 'L0_ffn_V2': _L0_ffn_in['V2'], 'L0_ffn_b1': _L0_ffn_in['b1'], 'L0_ffn_b2': _L0_ffn_in['b2']}

def reference(x, ctx_4096, L0_attn_q_weight, L0_attn_q_scale, L0_attn_k_weight, L0_attn_k_scale, L0_attn_v_weight, L0_attn_v_scale, L0_attn_o_weight, L0_attn_o_scale, L0_xattn_Wq_d, L0_xattn_W_qk, L0_xattn_Wkv_d, L0_xattn_Wv_u, L0_ffn_U1, L0_ffn_V1, L0_ffn_U2, L0_ffn_V2, L0_ffn_b1, L0_ffn_b2):
    import jax
    import jax.numpy as jnp

    def _L0_attn_ref(hidden_states, q_weight, q_scale, k_weight, k_scale, v_weight, v_scale, o_weight, o_scale):
        import jax, jax.numpy as jnp
        import numpy as np
        HIDDEN = 1024
        N_HEADS = 32
        N_KV_HEADS = 8
        HEAD_DIM = HIDDEN // N_HEADS
        N_REP = N_HEADS // N_KV_HEADS
        KV_DIM = N_KV_HEADS * HEAD_DIM

        def _kaiming_uniform(key, out_f, in_f):
            bound = 1.0 / np.sqrt(in_f)
            return jax.random.uniform(key, (out_f, in_f), jnp.float32, -bound, bound)

        def bitnet_linear(x, weight, scale_param):
            s = jnp.maximum(jnp.mean(jnp.abs(weight), axis=1), 1e-08)
            binary_w = jnp.sign(weight / s[:, None])
            y = jnp.einsum('bsi,oi->bso', x, binary_w)
            y = y * (s * scale_param)[None, None, :]
            return jnp.nan_to_num(y, nan=0.0, posinf=1000000.0, neginf=-1000000.0)
        b, s, _ = hidden_states.shape
        q = bitnet_linear(hidden_states, q_weight, q_scale)
        k = bitnet_linear(hidden_states, k_weight, k_scale)
        v = bitnet_linear(hidden_states, v_weight, v_scale)
        q = q.reshape(b, s, N_HEADS, HEAD_DIM).transpose(0, 2, 1, 3)
        k = k.reshape(b, s, N_KV_HEADS, HEAD_DIM).transpose(0, 2, 1, 3)
        v = v.reshape(b, s, N_KV_HEADS, HEAD_DIM).transpose(0, 2, 1, 3)
        k = jnp.repeat(k, N_REP, axis=1)
        v = jnp.repeat(v, N_REP, axis=1)
        scores = jnp.einsum('bhqd,bhkd->bhqk', q, k) / np.sqrt(HEAD_DIM)
        attn = jax.nn.softmax(scores, axis=-1)
        out = jnp.einsum('bhqk,bhkd->bhqd', attn, v)
        out = out.transpose(0, 2, 1, 3).reshape(b, s, HIDDEN)
        return bitnet_linear(out, o_weight, o_scale)

    def _L0_xattn_ref(Q, K, Wq_d, W_qk, Wkv_d, Wv_u):
        import jax, jax.numpy as jnp
        import numpy as np
        B, N, NKV = (2, 512, 512)
        E = 1024
        H = 16
        HD = E // H
        LQ = E // 8
        LKV = E // 16
        b, n, _ = Q.shape
        nkv = K.shape[1]
        C_q = Q @ Wq_d
        C_kv = K @ Wkv_d
        CqWqk = (C_q @ W_qk).reshape(b, n, H, LKV)
        scores = jnp.einsum('bnhl,bkl->bhnk', CqWqk, C_kv) / jnp.sqrt(jnp.asarray(LKV, dtype=Q.dtype))
        attn = jax.nn.softmax(scores, axis=-1)
        V_up = (C_kv @ Wv_u).reshape(b, nkv, H, HD)
        out = jnp.einsum('bhnk,bkhd->bnhd', attn, V_up)
        return out.reshape(b, n, H * HD)

    def _L0_ffn_ref(x, U1, V1, U2, V2, b1, b2):
        import jax, jax.numpy as jnp
        import numpy as np
        HIDDEN = 1024
        INTER = 2752
        RANK = 256
        B, S = (2, 512)
        P = jnp.einsum('bsh,hr->bsr', x, U1)
        H = jnp.einsum('bsr,rf->bsf', P, V1) + b1
        gate, up = (H[..., :INTER], H[..., INTER:])
        act = jax.nn.silu(gate) * up
        Z = jnp.einsum('bsi,ir->bsr', act, U2)
        out = jnp.einsum('bsr,rh->bsh', Z, V2) + b2
        return out
    x = x + _L0_attn_ref(_layernorm(x, axis=-1), L0_attn_q_weight, L0_attn_q_scale, L0_attn_k_weight, L0_attn_k_scale, L0_attn_v_weight, L0_attn_v_scale, L0_attn_o_weight, L0_attn_o_scale)
    x = x + _L0_xattn_ref(_layernorm(x, axis=-1), ctx_4096, L0_xattn_Wq_d, L0_xattn_W_qk, L0_xattn_Wkv_d, L0_xattn_Wv_u)
    x = x + _L0_ffn_ref(_layernorm(x, axis=-1), L0_ffn_U1, L0_ffn_V1, L0_ffn_U2, L0_ffn_V2, L0_ffn_b1, L0_ffn_b2)
    return x

_drawn_inputs = setup_inputs


def setup_inputs(seed=0):
    import zlib

    import numpy as np

    out = dict(_drawn_inputs(seed))
    spreads = {'L0_attn_q_scale': (1.0, 0.2),
     'L0_attn_k_scale': (1.0, 0.2),
     'L0_attn_v_scale': (1.0, 0.2),
     'L0_attn_o_scale': (1.0, 0.2)}
    factors = {}
    for name, (base, spread) in spreads.items():
        noise = np.random.default_rng([zlib.crc32(name.encode()), seed]).standard_normal(out[name].shape)
        drawn = base * np.exp(spread * noise) if base else spread * noise
        out[name] = jnp.asarray(drawn.astype(out[name].dtype))
    for name, factor in factors.items():
        out[name] = (out[name] * factor).astype(out[name].dtype)
    return out
```

```python
from contextlib import ExitStack

import concourse.bass as bass
from concourse import mybir

F32 = mybir.dt.float32
F32R = mybir.dt.float32r
F16 = mybir.dt.float16
ALU = mybir.AluOpType
ACT = mybir.ActivationFunctionType
AX = mybir.AxisListType

BATCH, SEQ, D = 8, 256, 1024
P = 128
TOK = BATCH * SEQ
KB = D // P
GT = 512
NG = TOK // GT
TILES = GT // P
GB = GT // SEQ
QT = SEQ // P
HEADS, KV_HEADS = 32, 8
HD = D // HEADS
REP = HEADS // KV_HEADS
KVD = KV_HEADS * HD
XH, XD = 16, 64
XPAIRS = XH // 2
LQ = 128
INTER, RANK = 2752, 256
RB = RANK // P
FB = (INTER + P - 1) // P
FLAST = INTER - (FB - 1) * P
LN_EPS = 1e-5
SIGN_EPS = 1e-8
ON_SCALAR = (1, 4, 6)


class Queues:

    ENGINES = ("tensor", "scalar", "vector", "gpsimd", "sync")

    def __init__(self, nc, ctx):
        self.nc, self.ctx = nc, ctx
        self.queue = {e: [] for e in self.ENGINES}
        self.done = {e: ctx.enter_context(nc.semaphore(f"{e}_done")) for e in self.ENGINES[:4]}
        self.count = {e: 0 for e in self.ENGINES}
        self.gate = {e: [] for e in self.ENGINES}
        self.lanes = []

    def op(self, engine, build, waits=(), signal=True):
        waits = self.gate[engine] + list(waits)
        self.gate[engine] = []
        token = None
        if signal:
            self.count[engine] += 1
            token = (self.done[engine], self.count[engine])
        self.queue[engine].append((waits, build, token and token[0], 1))
        return token

    def lane(self, name):
        lane = [self.ctx.enter_context(self.nc.semaphore(name)), 0]
        self.lanes.append(lane)
        return lane

    def dma(self, lane, out, in_, waits=()):
        waits = self.gate["sync"] + list(waits)
        self.gate["sync"] = []
        lane[1] += 16
        self.queue["sync"].append((waits, lambda e: e.dma_start(out, in_), lane[0], 16))
        return (lane[0], lane[1])

    def phase_end(self):
        last = [(self.done[e], self.count[e]) for e in self.ENGINES[:4] if self.count[e]]
        last += [(lane[0], lane[1]) for lane in self.lanes if lane[1]]
        for e in self.ENGINES:
            self.gate[e] = list(last)

    def emit(self, engine, eng):
        passed = {}
        for waits, build, sem, by in self.queue[engine]:
            for token in waits:
                if token is not None and passed.get(id(token[0]), 0) < token[1]:
                    eng.wait_ge(token[0], token[1])
                    passed[id(token[0])] = token[1]
            ins = build(eng)
            if sem is not None:
                ins.then_inc(sem, by)


class Ring:

    def __init__(self, bufs):
        self.bufs, self.users, self.n = bufs, [[] for _ in bufs], -1

    def take(self):
        self.n += 1
        k = self.n % len(self.bufs)
        assert self.n < len(self.bufs) or self.users[k], "taken before its last user was named"
        users, self.users[k] = self.users[k], []
        return self.bufs[k], users, k

    def used(self, k, *tokens):
        self.users[k] += tokens


def build_program(nc, x, ctx_in, wq, qs, wk, ks, wv, vs, wo, os_, wq_d, w_qk, wkv_d, wv_u,
                  u1, v1, u2, v2, b1, b2, out):
    ctx = ExitStack()
    q = Queues(nc, ctx)
    pe = lambda f, waits=(), signal=False: q.op("tensor", f, waits, signal)
    act = lambda f, waits=(), signal=True: q.op("scalar", f, waits, signal)
    dve = lambda f, waits=(), signal=True: q.op("vector", f, waits, signal)
    pool = lambda f, waits=(), signal=True: q.op("gpsimd", f, waits, signal)

    def sb(name, shape, dt, where=ctx):
        return where.enter_context(nc.sbuf_tensor(name, shape, dt))

    x1 = nc.dram_tensor("x1_scratch", [TOK, D], F32, kind="Internal").ap()
    x2 = nc.dram_tensor("x2_scratch", [TOK, D], F32, kind="Internal").ap()
    rows = lambda a, tile: a[tile * P:(tile + 1) * P, :]

    ident = sb("ident", [P, P], F32)
    ident16 = sb("ident16", [P, P], F16)
    ones = sb("ones", [P, P], F32)
    neg_half = sb("neg_half", [P, 1], F32)
    xin_bufs = [sb(f"xin{i}", [P, D], F32) for i in range(3)]
    prob = Ring([sb(f"prob{i}", [P, GT], F32) for i in range(3)])
    probT = Ring([sb(f"probT{i}", [P, GT], F32) for i in range(6)])
    tmp = Ring([sb(f"tmp{i}", [P, GT], F32) for i in range(2)])
    xin = Ring(xin_bufs)
    xin_lane = [q.lane(f"xin{i}_loaded") for i in range(3)]
    bn = Ring([sb(f"bn{i}", [P, 16], F32) for i in range(4)])
    maxes = Ring([sb(f"maxes{i}", [P, 4], F32) for i in range(4)])
    row_sums = Ring([sb(f"row_sums{i}", [P, 4, REP], F32) for i in range(3)])

    bank = [ctx.enter_context(nc.psum_tensor(f"bank{i}", [P, GT], F32)) for i in range(8)]
    scores = Ring(bank[0:3])
    turned = Ring(bank[3:5])
    attn = Ring(bank[5:6])
    proj = Ring(bank[6:8])

    c0 = pool(lambda e: e.memset(ident[:, :], 0.0))
    c1 = pool(lambda e: e.affine_select(out=ident[:, :], in_=ident[:, :], compare_op=ALU.not_equal, fill=1.0,
                                        base=0, pattern=[[-1, P]], channel_multiplier=1), [c0])
    ident_ok = pool(lambda e: e.tensor_copy(ident16[:, :], ident[:, :]), [c1])
    ones_ok = pool(lambda e: e.memset(ones[:, :], 1.0))
    half_ok = pool(lambda e: e.memset(neg_half[:, :], -0.5))

    def load_rows(src, waits=()):
        buf, users, k = xin.take()
        return buf, k, q.dma(xin_lane[k], buf[:, :], src, list(users) + list(waits))

    def layernorm(buf, k, loaded):
        st, users, sk = bn.take()
        t = [dve(lambda e, i=i: e.bn_stats(st[:, 6 * i:6 * i + 6], buf[:, GT * i:GT * (i + 1)]),
                 [loaded] + users) for i in range(2)]
        t = dve(lambda e: e.bn_aggr(st[:, 12:14], st[:, 0:12]), t)
        dve(lambda e: e.tensor_scalar(st[:, 12:13], st[:, 12:13], -1.0, None, ALU.mult), [t], False)
        t = dve(lambda e: e.tensor_scalar(st[:, 14:15], st[:, 13:14], LN_EPS, None, ALU.add), [t])
        t = pool(lambda e: e.tensor_tensor(st[:, 15:16], st[:, 14:15], neg_half[:, :], ALU.pow), [t, half_ok])
        t = pool(lambda e: e.tensor_scalar(buf[:, :], buf[:, :], st[:, 12:13], st[:, 15:16], ALU.add, ALU.mult), [t])
        bn.used(sk, t)
        return t

    def transpose_tile(src, ready, hi, lo, m, waits, used):
        pieces = []
        for half in range(2):
            def mm(half=half):
                J, users, jk = proj.take()
                for i in range(4):
                    kb = 4 * half + i
                    t = pe(lambda e, i=i, kb=kb: e.transpose(J[:, i * P:(i + 1) * P], src[:, kb * P:(kb + 1) * P],
                                                             ident[:, :]),
                           [ready, ident_ok] + users, signal=i == 3)
                used(t)

                def split():
                    J3 = J[:, :].rearrange("p (k n) -> p k n", k=4)
                    dst = lambda a: a[:, 4 * half:4 * half + 4, m * P:(m + 1) * P]
                    th = act(lambda e: e.activation(dst(hi), J3, ACT.Copy), [t] + waits)
                    tl = dve(lambda e: e.tensor_tensor(dst(lo), J3, as_f32(dst(hi)), ALU.subtract), [th] + waits)
                    proj.used(jk, tl)
                    return [th, tl]
                return split
            pieces.append(mm)
        return pieces

    def as_f32(a):
        return a.bitcast(F32) if a.dtype == F32R else a

    def run(piece):
        rest = piece()
        return rest() if rest else None

    def score_stage(mms, scale):
        S, users, sk = scores.take()
        t = mms(S, users)
        mx, mu, mk = maxes.take()
        S3 = S[:, :].rearrange("p (a b) -> p a b", a=QT)
        t = dve(lambda e: e.tensor_reduce(mx[:, 0:QT], S3, AX.X, ALU.max), [t] + mu)
        t = dve(lambda e: e.tensor_scalar(mx[:, QT:2 * QT], mx[:, 0:QT], -scale, None, ALU.mult), [t])
        return S, sk, mx, mk, t

    def exp_stage(S, sk, mx, mk, t, scale, sums):
        Pb, pu, pk = prob.take()
        te = [act(lambda e, a=a, total=sums(a): e.activation(
                      Pb[:, a * SEQ:(a + 1) * SEQ], S[:, a * SEQ:(a + 1) * SEQ], ACT.Exp,
                      bias=mx[:, QT + a:QT + a + 1], scale=scale, accum_out=total),
                  [t] + pu) for a in range(QT)]
        scores.used(sk, te[-1])
        maxes.used(mk, te[-1])
        return Pb, pk, te

    def turn_stage(Pb, pk, te):
        T, users, tk = turned.take()
        for kt in range(QT):
            for qt in range(QT):
                t = pe(lambda e, kt=kt, qt=qt: e.transpose(
                    T[:, kt * SEQ + qt * P:kt * SEQ + (qt + 1) * P],
                    Pb[:, qt * SEQ + kt * P:qt * SEQ + (kt + 1) * P], ident[:, :]),
                    te + users, signal=kt == QT - 1 and qt == QT - 1)
        prob.used(pk, t)
        return T, tk, t

    def evac_stage(T, tk, t, n):
        PT, ptu, ptk = probT.take()
        if n % 8 in ON_SCALAR:
            t = act(lambda e: e.activation(PT[:, :], T[:, :], ACT.Copy), [t] + ptu)
        else:
            t = dve(lambda e: e.tensor_copy(PT[:, :], T[:, :]), [t] + ptu)
        turned.used(tk, t)
        return PT, ptk, t

    AHEAD = 3

    def attention(units, side_work):
        heads = [(u, i) for u in units for i in range(u["heads"])]
        scored, soft, ready, rest = {}, {}, {}, []

        def score(n):
            if n < len(heads):
                u, i = heads[n]
                if i == 0:
                    u.update(u.pop("make")())
                    u["begin"]()
                scored[n] = score_stage(lambda S, w: u["scores"](i, S, w), u["scale"])

        def exp(n):
            if n < len(heads):
                u, i = heads[n]
                soft[n] = exp_stage(*scored.pop(n), u["scale"], lambda a: u["sums"](i, a))
                u["box"]["exp"] = soft[n][2][-1]

        for n in range(AHEAD):
            score(n)
        exp(0)
        for n in range(len(heads) + 1):
            if n < len(heads):
                T = turn_stage(*soft.pop(n))
                exp(n + 1)
                ready[n] = evac_stage(*T, n)
            for r in rest:
                r()
            rest = []
            for piece in side_work(n):
                r = piece()
                if r:
                    rest.append(r)
            score(n + AHEAD)
            if n >= 1:
                u, i = heads[n - 1]
                s = u["set"]
                if i % s == s - 1:
                    u["values"](i // s, [ready.pop(n - s + j) for j in range(s)])
                if i == u["heads"] - 1:
                    u["end"]()
        for r in rest:
            r()

    mem = ExitStack()
    sW = sb("signs_qkv", [P, KB, D + 2 * KVD], F16, mem)
    sWo = sb("signs_o", [P, KB, D], F32R, mem)
    NSC = (2 * D + 2 * KVD) // P
    QB, VB, OB = KB, KB + KVD // P, KB + 2 * KVD // P
    sc_rows = sb("scale_rows", [NSC, P], F32, mem)
    sc = sb("scale_cols", [P, NSC], F32, mem)
    abs_sum = sb("abs_sum", [P, NSC], F32, mem)
    s_mean = sb("s_mean", [P, NSC], F32, mem)
    s_inv = sb("s_inv", [P, NSC], F32, mem)
    chan = sb("channel_scale", [P, NSC], F32, mem)
    cv = sb("v_scale_all", [P, KVD], F32, mem)
    co = sb("o_scale_all", [P, D], F32, mem)
    sign_ring = Ring([sb("sign0", [P, D], F16, mem)])
    hT_hi = sb("hT_hi", [P, KB, GT], F16, mem)
    hT_lo = sb("hT_lo", [P, KB, GT], F16, mem)
    kst = sb("k_stack", [P, KV_HEADS, GT], F32R, mem)
    vall = sb("v_all", [P, TILES, KVD], F32, mem)
    hl = Ring([sb(f"hi_lo{i}", [P, 2, GT], F32R, mem) for i in range(2)])
    qst = Ring([sb(f"q_stack{i}", [P, REP, GT], F32R, mem) for i in range(3)])
    OT_hi = sb("attnT_hi", [P, KB, GT], F32R, mem)
    OT_lo = sb("attnT_lo", [P, KB, GT], F32R, mem)
    r_all = sb("recip_all", [P, 4, REP, HD], F32, mem)
    R_sb = sb("recipT", [P, GT], F32, mem)
    OTn = sb("attnT", [P, GT], F32, mem)
    sc_lane = q.lane("scales_loaded")
    st_lanes = [q.lane(f"stack{i}_loaded") for i in range(3)]
    k_lanes = [q.lane(f"k_stack{i}_loaded") for i in range(2)]
    x1_lanes = [q.lane(f"x1_stored{i}") for i in range(3)]

    zeroed = [pool(lambda e, a=a: e.memset(a[:, :, :].bitcast(F32), 0.0)) for a in [kst] + qst.bufs]

    t = None
    for src, n, at in ((qs, KB, 0), (ks, KVD // P, QB), (vs, KVD // P, VB), (os_, KB, OB)):
        t = q.dma(sc_lane, sc_rows[at:at + n, :], src.rearrange("(a b) -> a b", b=P))
    J, users, jk = proj.take()
    t = pe(lambda e: e.transpose(J[:, 0:NSC], sc_rows[:, :], ident[0:NSC, 0:NSC]), [t, ident_ok], True)
    sc_ok = dve(lambda e: e.tensor_copy(sc[:, :], J[:, 0:NSC]), [t])
    proj.used(jk, sc_ok)

    chan_ok = {}
    signs_ok = {}

    def sign_piece(src, tile, idx, dst, at):
        buf, k, loaded = load_rows(rows(src, tile))
        sg, sgu, sgk = sign_ring.take()
        c = slice(idx, idx + 1)
        t = act(lambda e: e.activation(sg[:, :], buf[:, :], ACT.Abs, accum_out=abs_sum[:, c]), [loaded] + sgu)
        t = dve(lambda e: e.tensor_scalar(s_mean[:, c], abs_sum[:, c], 1.0 / D, SIGN_EPS, ALU.mult, ALU.max), [t])
        ti = dve(lambda e: e.reciprocal(s_inv[:, c], s_mean[:, c]), [t])
        chan_ok[idx] = dve(lambda e: e.tensor_tensor(chan[:, c], s_mean[:, c], sc[:, c], ALU.mult), [t, sc_ok])
        t = act(lambda e: e.activation(sg[:, :], buf[:, :], ACT.Sign, scale=s_inv[:, c]), [ti])
        xin.used(k, t)

        def mm():
            J, users, jk = proj.take()
            J16 = J[:, :].bitcast(F16)
            for kb in range(KB):
                tt = pe(lambda e, kb=kb: e.transpose(J16[:, kb * P:(kb + 1) * P], sg[:, kb * P:(kb + 1) * P],
                                                     ident16[:, :]), [t, ident_ok] + users, kb == KB - 1)
            sign_ring.used(sgk, tt)

            def evac():
                J3 = J16.rearrange("p (k n) -> p k n", k=KB)
                signs_ok[idx] = dve(lambda e: e.tensor_copy(dst[:, :, at:at + P], J3), [tt])
                proj.used(jk, signs_ok[idx])
            return evac
        return mm

    def scale_all(first, n, dst):
        last = None
        for half in range((n + 3) // 4):
            J, users, jk = proj.take()
            m = min(4, n - 4 * half)
            for i in range(m):
                idx = first + 4 * half + i
                dg, du, dk = tmp.take()
                t = dve(lambda e, idx=idx, dg=dg: e.tensor_scalar(dg[:, 0:P], ident[:, :], chan[:, idx:idx + 1], None,
                                                                  ALU.mult), [chan_ok[idx], ident_ok] + du)
                t = pe(lambda e, i=i, dg=dg, J=J: e.matmul(J[:, i * P:(i + 1) * P], ones[:, :], dg[:, 0:P],
                                                           start=True, stop=True), [t, ones_ok] + users, True)
                tmp.used(dk, t)
            last = dve(lambda e, half=half, m=m, J=J: e.tensor_copy(dst[:, half * GT:half * GT + m * P],
                                                                    J[:, 0:m * P]), [t])
            proj.used(jk, last)
        return last

    hT_users = []
    hT_ready = []
    kst_users, v_users, OT_users = [], [], []

    def ln_pieces(g, src, hi, lo, stored=()):
        out_pieces = []
        users = list(hT_users)
        hT_users.clear()
        hT_ready.clear()
        for m in range(TILES):
            def first(m=m):
                buf, k, loaded = load_rows(rows(src, g * TILES + m), stored)
                return transpose_tile(buf, layernorm(buf, k, loaded), hi, lo, m, users, lambda t: xin.used(k, t))
            box = {}

            def a(first=first, box=box):
                box["p"] = first()
                r = box["p"][0]()
                return lambda: hT_ready.extend(r())

            def b(box=box):
                r = box["p"][1]()
                return lambda: hT_ready.extend(r())
            out_pieces += [a, b]
        return out_pieces

    def project_split(col, idx, J, users):
        for kb in range(KB):
            for part in (hT_hi, hT_lo):
                t = pe(lambda e, kb=kb, part=part: e.matmul(
                    J[:, :], sW[:, kb, col:col + P], part[:, kb, :],
                    start=kb == 0 and part is hT_hi, stop=kb == KB - 1 and part is hT_lo),
                    hT_ready + users + [signs_ok[idx]], kb == KB - 1 and part is hT_lo)
        hT_users.append(t)
        return t

    def split_scaled(J, jk, t, idx):
        b, bu, bk = hl.take()
        c = chan[:, idx:idx + 1]
        th = act(lambda e: e.activation(b[:, 0, :], J[:, :], ACT.Copy, scale=c), [t, chan_ok[idx]] + bu)
        tl = dve(lambda e: e.scalar_tensor_tensor(b[:, 1, :], J[:, :], c, b[:, 0, :].bitcast(F32),
                                                  ALU.mult, ALU.subtract), [th, chan_ok[idx]] + bu)
        proj.used(jk, tl)
        return b, bk, th, tl

    kst_ready = {}

    def k_piece(kt):
        def mm():
            J, users, jk = proj.take()
            t = project_split(D + kt * P, QB + kt, J, users)

            def rest():
                b, bk, th, tl = split_scaled(J, jk, t, QB + kt)
                lane = k_lanes[kt]
                for part, tok, at in ((0, th, (0, 1)), (1, tl, (2,))):
                    for a in at:
                        for i in range(P // HD):
                            t2 = q.dma(lane, kst[a * HD:(a + 1) * HD, kt * (P // HD) + i, :].bitcast(F32),
                                       b[i * HD:(i + 1) * HD, part, :].bitcast(F32), [tok] + kst_users + zeroed)
                hl.used(bk, t2)
                kst_ready[kt] = t2
            return rest
        return mm

    v_ready = []

    def v_piece(pair):
        def mm():
            J, users, jk = proj.take()
            for i in range(2):
                m = 2 * pair + i
                for kb in range(KB):
                    for part in (hT_hi, hT_lo):
                        last = kb == KB - 1 and part is hT_lo
                        t = pe(lambda e, i=i, m=m, kb=kb, part=part, last=last: e.matmul(
                            J[:, i * KVD:(i + 1) * KVD], part[:, kb, m * P:(m + 1) * P], sW[:, kb, D + KVD:D + 2 * KVD],
                            start=kb == 0 and part is hT_hi, stop=last),
                            hT_ready + users + [signs_ok[VB], signs_ok[VB + 1]], last and i == 1)
            hT_users.append(t)

            def rest():
                cvb = cv[:, :].rearrange("p (o n) -> p o n", o=1).to_broadcast([P, 2, KVD])
                t2 = dve(lambda e: e.tensor_tensor(vall[:, 2 * pair:2 * pair + 2, :],
                                                   J[:, :].rearrange("p (o n) -> p o n", o=2), cvb, ALU.mult),
                         [t, cv_ok[0]] + v_users)
                proj.used(jk, t2)
                v_ready.append(t2)
            return rest
        return mm

    q_ready = {}

    def q_pieces(g, tq, n_chunks=4):
        box = {}

        def chunk(c):
            if c == 0:
                box["J"] = proj.take()
            J, users, jk = box["J"]
            for kb in range(c * KB // n_chunks, (c + 1) * KB // n_chunks):
                for part in (hT_hi, hT_lo):
                    last = kb == KB - 1 and part is hT_lo
                    t = pe(lambda e, kb=kb, part=part, last=last: e.matmul(
                        J[:, :], sW[:, kb, tq * P:(tq + 1) * P], part[:, kb, :],
                        start=kb == 0 and part is hT_hi, stop=last), hT_ready + users + [signs_ok[tq]], last)
            if c < n_chunks - 1:
                return None
            hT_users.append(t)

            def rest():
                b, bk, th, tl = split_scaled(J, jk, t, tq)
                st, su, sk = qst.take()
                lane = st_lanes[sk]
                for part, tok, at in ((0, th, (0, 2)), (1, tl, (1,))):
                    for a in at:
                        for i in range(REP):
                            t2 = q.dma(lane, st[a * HD:(a + 1) * HD, i, :].bitcast(F32),
                                       b[i * HD:(i + 1) * HD, part, :].bitcast(F32), [tok] + su + zeroed)
                hl.used(bk, t2)
                q_ready[g, tq] = (st, sk, t2)
            return rest
        return [lambda c=c: chunk(c) for c in range(n_chunks)]

    OT_ready = []

    def self_unit(g, tq):
        u = {"heads": GB * REP, "scale": HD ** -0.5, "set": REP}
        box = {}

        def begin():
            box["q"] = q_ready[g, tq]
            box["sums"], box["su"], box["sk"] = row_sums.take()

        def mk_scores(i, S, waits):
            b, r = divmod(i, REP)
            st, sk, ready = box["q"]
            for a in range(QT):
                t = pe(lambda e, a=a: e.matmul(S[:, a * SEQ:(a + 1) * SEQ],
                                               st[:, r, b * SEQ + a * P:b * SEQ + (a + 1) * P],
                                               kst[:, tq, b * SEQ:(b + 1) * SEQ], start=True, stop=True),
                       waits + zeroed + [ready, kst_ready[tq // (P // HD)]] + box["su"], a == QT - 1)
            if i == GB * REP - 1:
                qst.used(sk, t)
                kst_users.append(t)
            return t

        def sums(i, a):
            b, r = divmod(i, REP)
            return box["sums"][:, b * QT + a, r:r + 1]

        def values(b, pts):
            if b == 0:
                box["O"], box["ou"], box["ok"] = attn.take()
            O = box["O"]
            for kt in range(QT):
                for r in range(REP):
                    PT, ptk, tp = pts[r]
                    t = pe(lambda e, kt=kt, r=r, PT=PT: e.matmul(
                        O[r * HD:(r + 1) * HD, b * SEQ:(b + 1) * SEQ], vall[:, b * QT + kt, tq * HD:(tq + 1) * HD],
                        PT[:, kt * SEQ:(kt + 1) * SEQ], start=kt == 0, stop=kt == QT - 1,
                        tile_position=(0, r * HD)), [tp] + v_ready + box["ou"], kt == QT - 1)
                    if kt == QT - 1:
                        probT.used(ptk, t)
            box["o_t"] = t

        def end():
            s = box["sums"]
            t = dve(lambda e: e.reciprocal(s[:, :, :], s[:, :, :]), [box["exp"]])
            t = pool(lambda e: e.tensor_scalar(
                r_all[:, :, :, :].rearrange("p a r d -> p (a r) d"),
                s[:, :, :].rearrange("p a (r o) -> p (a r) o", o=1).to_broadcast([P, 4 * REP, HD]),
                1.0, 0.0, ALU.mult, ALU.add), [t] + r_users)
            r_users.clear()
            row_sums.used(box["sk"], t)
            J, users, jk = proj.take()
            for a in range(4):
                t2 = pe(lambda e, a=a: e.transpose(J[:, a * P:(a + 1) * P],
                                                   r_all[:, a, :, :].rearrange("p r d -> p (r d)"), ident[:, :]),
                        [t] + users, a == 3)
            r_users.append(t2)
            t3 = act(lambda e: e.activation(R_sb[:, :], J[:, :], ACT.Copy), [t2] + R_users)
            proj.used(jk, t3)
            t4 = dve(lambda e: e.tensor_tensor(OTn[:, :], box["O"][:, :], R_sb[:, :], ALU.mult),
                     [t3, box["o_t"]] + OTn_users)
            R_users[:] = [t4]
            attn.used(box["ok"], t4)
            t5 = pool(lambda e: e.tensor_scalar(OT_hi[:, tq, :], OTn[:, :], 1.0, 0.0, ALU.mult, ALU.add),
                      [t4] + OT_users)
            t6 = pool(lambda e: e.tensor_tensor(OT_lo[:, tq, :], OTn[:, :], OT_hi[:, tq, :].bitcast(F32),
                                                ALU.subtract), [t5] + OT_users)
            OTn_users[:] = [t6]
            OT_ready.append(t6)
            if tq == KV_HEADS - 1:
                v_users.clear()
                v_users.append(box["o_t"])
        u.update(begin=begin, scores=mk_scores, sums=sums, values=values, end=end, box=box)
        return u

    r_users, R_users, OTn_users = [], [], []

    def o_pieces(g):
        pieces = []
        ready = []
        for m in range(TILES):
            box = {}
            for n in range(2):
                def mm(m=m, n=n, box=box):
                    if n == 0:
                        box["x"], box["k"], box["xl"] = load_rows(rows(x, g * TILES + m))
                        box["ready"] = list(OT_ready)
                    J, users, jk = proj.take()
                    for tq in range(KB):
                        for part in (OT_hi, OT_lo):
                            last = tq == KB - 1 and part is OT_lo
                            t = pe(lambda e, tq=tq, part=part, last=last: e.matmul(
                                J[:, :], part[:, tq, m * P:(m + 1) * P], sWo[:, tq, n * GT:(n + 1) * GT],
                                start=tq == 0 and part is OT_hi, stop=last),
                                box["ready"] + users + [signs_ok[OB + i] for i in range(KB)], last)
                    if m == TILES - 1 and n == 1:
                        OT_users[:] = [t]
                        OT_ready.clear()

                    def rest():
                        y, yu, yk = tmp.take()
                        xs = box["x"][:, n * GT:(n + 1) * GT]
                        t2 = dve(lambda e: e.tensor_tensor(y[:, :], J[:, :], co[:, n * GT:(n + 1) * GT], ALU.mult),
                                 [t, co_ok[0]] + yu)
                        proj.used(jk, t2)
                        t3 = dve(lambda e: e.tensor_tensor(xs, xs, y[:, :], ALU.add), [t2, box["xl"]])
                        tmp.used(yk, t3)
                        if n == 1:
                            t4 = q.dma(x1_lanes[box["k"]], rows(x1, g * TILES + m), box["x"][:, :], [t3])
                            xin.used(box["k"], t4)
                            x1_stored[g * TILES + m] = t4
                    return rest
                pieces.append(mm)
        return pieces

    x1_stored = {}
    cv_ok, co_ok = [None], [None]

    for src, n, first, at in ((wk, KVD // P, QB, D), (wv, KVD // P, VB, D + KVD)):
        for i in range(n):
            run(sign_piece(src, i, first + i, sW, at + i * P))
    cv_ok[0] = scale_all(VB, KVD // P, cv)
    for i in range(3):
        run(sign_piece(wq, i, i, sW, i * P))

    for piece in ln_pieces(0, x, hT_hi, hT_lo):
        run(piece)
    for g in range(NG):
        v_ready.clear()
        for kt in range(KVD // P):
            run(k_piece(kt))
        kst_users.clear()
        for c in q_pieces(g, 0):
            run(c)
        for pair in range(TILES // 2):
            run(v_piece(pair))
        for c in q_pieces(g, 1):
            run(c)
        units = [{"heads": GB * REP, "make": lambda tq=tq, g=g: self_unit(g, tq)} for tq in range(KV_HEADS)]
        queries = {}

        def side_work(n, g=g, queries=queries):
            u, i = divmod(n, GB * REP)
            if u + 2 < KV_HEADS and i < 4:
                if i == 0:
                    queries[u] = q_pieces(g, u + 2)
                return [queries[u][i]]
            if g == 0 and u + 3 < KB and i == 5:
                return [sign_piece(wq, u + 3, u + 3, sW, (u + 3) * P)]
            if g == 0 and u < KB and i == 7:
                return [sign_piece(wo, u, OB + u, sWo, u * P)]
            return []
        attention(units, side_work)
        if g == 0:
            co_ok[0] = scale_all(OB, KB, co)
        o_work = o_pieces(g)
        ln_work = ln_pieces(g + 1, x, hT_hi, hT_lo) if g + 1 < NG else []
        for i, piece in enumerate(o_work):
            if ln_work:
                run(ln_work[i])
            run(piece)
    q.phase_end()
    mem.close()

    mem = ExitStack()
    actT = Ring([(sb(f"actT_hi{i}", [P, KB, GT], F32R, mem), sb(f"actT_lo{i}", [P, KB, GT], F32R, mem))
                 for i in range(2)])
    wqd = [sb(f"wq_down_{n}", [P, KB, LQ], F32R, mem) for n in ("hi", "lo")]
    wqk = [sb(f"w_qk_{n}", [P, XH * XD], F32R, mem) for n in ("hi", "lo")]
    wkv = [sb(f"wkv_down_{n}", [P, KB, 2, XD], F32R, mem) for n in ("hi", "lo")]
    wvu = sb("wv_up", [P, XH * XD], F32R, mem)
    cq = sb("cq_hi_lo", [P, 2, GT], F32R, mem)
    ckv = Ring([sb(f"ckv{i}", [P, 2, GT], F32R, mem) for i in range(2)])
    xv = sb("xv_all", [P, TILES, XH * XD], F32, mem)
    hl = Ring([sb(f"xhi_lo{i}", [P, 2, GT], F32R, mem) for i in range(2)])
    xst = Ring([sb(f"xq_stack{i}", [P, 2, GT], F32R, mem) for i in range(3)])
    xg = sb("x_group", [P, TILES, D], F32, mem)
    OTs = Ring([sb(f"xattnT{i}", [P, GT], F32, mem) for i in range(2)])
    xr = Ring([sb(f"xrecip{i}", [P, 4, 2], F32, mem) for i in range(2)])
    xst_lanes = [q.lane(f"xq_stack{i}_loaded") for i in range(3)]
    xg_lane, x2_lane = q.lane("x_group_loaded"), q.lane("x2_stored")

    def split_weight(src_ap, hi, lo, shape_view, waits):
        th = pool(lambda e: e.tensor_scalar(hi, shape_view, 1.0, 0.0, ALU.mult, ALU.add), waits)
        tl = dve(lambda e: e.tensor_tensor(lo, shape_view, hi.bitcast(F32), ALU.subtract), [th])
        return [th, tl]

    def load_into(src, view, waits=()):
        buf, users, k = xin.take()
        return buf, k, q.dma(xin_lane[k], view(buf), src, list(users) + list(waits))

    buf, k, t = load_into(wq_d.rearrange("(k p) n -> p k n", p=P),
                          lambda b: b[:, :].rearrange("p (k n) -> p k n", k=KB))
    wqd_ok = split_weight(None, wqd[0][:, :, :], wqd[1][:, :, :], buf[:, :].rearrange("p (k n) -> p k n", k=KB), [t])
    xin.used(k, *wqd_ok)
    buf, k, t = load_into(w_qk, lambda b: b[:, :])
    wqk_ok = split_weight(None, wqk[0][:, :], wqk[1][:, :], buf[:, :], [t])
    xin.used(k, *wqk_ok)
    buf, k, t = load_into(wkv_d.rearrange("(k p) n -> p k n", p=P),
                          lambda b: b[:, 0:KB * XD].rearrange("p (k n) -> p k n", k=KB))
    view = buf[:, 0:KB * XD].rearrange("p (k n) -> p k n", k=KB)
    wkv_ok = []
    for c in range(2):
        wkv_ok += split_weight(None, wkv[0][:, :, c, :], wkv[1][:, :, c, :], view, [t])
    xin.used(k, *wkv_ok)
    buf, k, t = load_into(wv_u, lambda b: b[0:XD, :])
    t2 = q.dma(xin_lane[k], buf[XD:P, :], wv_u)
    t = pool(lambda e, buf=buf: e.tensor_scalar(wvu[:, :], buf[:, :], 1.0, 0.0, ALU.mult, ALU.add), [t, t2])
    wvu_ok = dve(lambda e, buf=buf: e.tensor_tensor(wvu[XD:P, :], buf[XD:P, :], wvu[XD:P, :].bitcast(F32),
                                                    ALU.subtract), [t])
    xin.used(k, wvu_ok)

    def split_bank(J, jk, t, hi, lo, waits):
        th = act(lambda e: e.activation(hi, J[:, :], ACT.Copy), [t] + waits)
        tl = dve(lambda e: e.tensor_tensor(lo, J[:, :], hi.bitcast(F32), ALU.subtract), [th] + waits)
        proj.used(jk, tl)
        return [th, tl]

    def down_three(J, users, w, parts, ready):
        n = 0
        for kb in range(KB):
            for wp, ap in ((0, 0), (0, 1), (1, 0)):
                last = kb == KB - 1 and wp == 1
                t = pe(lambda e, kb=kb, wk=w(wp, kb), ap=ap, first=n == 0, last=last: e.matmul(
                    J[:, :], wk, parts[ap][:, kb, :], start=first, stop=last), ready + users, last)
                n += 1
        return t

    def turned_group(g, src, waits_of, normed):
        parts, users, ak = actT.take()
        ready = []
        for m in range(TILES):
            buf, k, loaded = load_rows(rows(src, g * TILES + m), waits_of(g * TILES + m))
            ok = layernorm(buf, k, loaded) if normed else loaded
            pieces = transpose_tile(buf, ok, parts[0], parts[1], m, users, lambda t, k=k: xin.used(k, t))
            for p in pieces:
                ready += run(p)
        return parts, ak, ready

    cq_users, xv_users, xg_users = [], [], []
    x2_stored = {}

    def cross_unit(j, kv, kvk, kv_ok, v_ok, group, n_heads=2 * GB):
        box = {}
        st, sk, ready = group["q"][j]

        def begin():
            box["sums"], box["su"], box["sk"] = row_sums.take()

        def mk_scores(i, S, waits):
            b, r = divmod(i, 2)
            for a in range(QT):
                for part in range(2):
                    t = pe(lambda e, a=a, part=part: e.matmul(
                        S[:, a * SEQ:(a + 1) * SEQ], st[:, r, b * SEQ + a * P:b * SEQ + (a + 1) * P],
                        kv[:, part, b * SEQ:(b + 1) * SEQ], start=part == 0, stop=part == 1),
                        waits + [ready] + kv_ok + box["su"], a == QT - 1 and part == 1)
            if i == n_heads - 1:
                xst.used(sk, t)
                if j == XPAIRS - 1:
                    ckv.used(kvk, t)
            return t

        def sums(i, a):
            b, r = divmod(i, 2)
            return box["sums"][:, b * QT + a, r:r + 1]

        def values(b, pts):
            if b == 0:
                box["O"], box["ou"], box["ok"] = attn.take()
            O = box["O"]
            for kt in range(QT):
                for r in range(2):
                    PT, ptk, tp = pts[r]
                    t = pe(lambda e, kt=kt, r=r, PT=PT: e.matmul(
                        O[r * XD:(r + 1) * XD, b * SEQ:(b + 1) * SEQ],
                        xv[:, b * QT + kt, (2 * j + r) * XD:(2 * j + r + 1) * XD],
                        PT[:, kt * SEQ:(kt + 1) * SEQ], start=kt == 0, stop=kt == QT - 1,
                        tile_position=(0, r * XD)), [tp] + v_ok + box["ou"], kt == QT - 1)
                    if kt == QT - 1:
                        probT.used(ptk, t)
            box["o_t"] = t
            if j == XPAIRS - 1:
                xv_users[:] = [t]

        def end():
            rc, ru, rk = xr.take()
            tr = dve(lambda e: e.reciprocal(rc[:, :, :], box["sums"][:, :, 0:2]), [box["exp"]] + ru)
            row_sums.used(box["sk"], tr)
            o, ou, ok = OTs.take()
            t = act(lambda e: e.activation(o[:, :], box["O"][:, :], ACT.Copy), [box["o_t"]] + ou)
            attn.used(box["ok"], t)
            J, users, jk = proj.take()
            for a in range(TILES):
                t2 = pe(lambda e, a=a: e.transpose(J[:, a * P:(a + 1) * P], o[:, a * P:(a + 1) * P], ident[:, :]),
                        [t] + users, a == TILES - 1)
            OTs.used(ok, t2)
            y, yu, yk = tmp.take()
            heads4 = lambda a: a.rearrange("p (a r d) -> p a r d", a=TILES, r=2)
            t3 = dve(lambda e: e.tensor_tensor(
                heads4(y[:, :]), heads4(J[:, :]),
                rc[:, :, :].rearrange("p a (r o) -> p a r o", o=1).to_broadcast([P, TILES, 2, XD]), ALU.mult),
                [t2, tr] + yu)
            proj.used(jk, t3)
            xr.used(rk, t3)
            xs = xg[:, :, j * P:(j + 1) * P]
            t4 = pool(lambda e: e.tensor_tensor(xs, xs, y[:, :].rearrange("p (a n) -> p a n", a=TILES), ALU.add),
                      [t3, group["xl"]])
            tmp.used(yk, t4)
            group["x_done"] = t4
        return dict(heads=n_heads, scale=XD ** -0.5, set=2, box=box, begin=begin, scores=mk_scores, sums=sums,
                    values=values, end=end)

    for g in range(NG):
        group = {"q": {}}
        group["xl"] = q.dma(xg_lane, xg[:, :, :], x1[g * GT:(g + 1) * GT, :].rearrange("(a p) n -> p a n", p=P),
                            [x1_stored[g * TILES + m] for m in range(TILES)] + xg_users)
        parts, ak, ready = turned_group(g, x1, lambda i: [x1_stored[i]], True)
        J, users, jk = proj.take()
        t = down_three(J, users, lambda wp, kb: wqd[wp][:, kb, :], parts, ready + wqd_ok)
        actT.used(ak, t)
        cq_ok = split_bank(J, jk, t, cq[:, 0, :], cq[:, 1, :], cq_users)
        parts, ak, ready = turned_group(g, ctx_in, lambda i: [], False)
        J, users, jk = proj.take()
        t = down_three(J, users, lambda wp, kb: wkv[wp][:, kb, :, :].rearrange("p c n -> p (c n)"), parts,
                       ready + wkv_ok)
        actT.used(ak, t)
        kv, ku, kvk = ckv.take()
        kv_ok = split_bank(J, jk, t, kv[:, 0, :], kv[:, 1, :], ku)
        v_ok = []
        for m in range(TILES):
            for n in range(2):
                J, users, jk = proj.take()
                for part in range(2):
                    t = pe(lambda e, J=J, part=part, m=m, n=n, kv=kv: e.matmul(
                        J[:, :], kv[:, part, m * P:(m + 1) * P], wvu[:, n * GT:(n + 1) * GT],
                        start=part == 0, stop=part == 1), kv_ok + [wvu_ok] + users, part == 1)
                cp = act if n else dve
                f = ((lambda e, J=J, m=m, n=n: e.activation(xv[:, m, n * GT:(n + 1) * GT], J[:, :], ACT.Copy)) if n else
                     (lambda e, J=J, m=m, n=n: e.tensor_copy(xv[:, m, n * GT:(n + 1) * GT], J[:, :])))
                t = cp(f, [t] + xv_users)
                proj.used(jk, t)
                v_ok.append(t)

        def xq_piece(j, group=group, cq_ok=cq_ok):
            def mm():
                J, users, jk = proj.take()
                for n, (wp, ap) in enumerate(((0, 0), (0, 1), (1, 0))):
                    t = pe(lambda e, wp=wp, ap=ap, n=n: e.matmul(
                        J[:, :], wqk[wp][:, j * P:(j + 1) * P], cq[:, ap, :], start=n == 0, stop=n == 2),
                        cq_ok + wqk_ok + users, n == 2)
                if j == XPAIRS - 1:
                    cq_users[:] = [t]

                def rest():
                    b, bu, bk = hl.take()
                    th, tl = split_bank(J, jk, t, b[:, 0, :], b[:, 1, :], bu)
                    st, su, sk = xst.take()
                    for part, tok in ((0, th), (1, tl)):
                        for r in range(2):
                            t2 = q.dma(xst_lanes[sk], st[part * XD:(part + 1) * XD, r, :].bitcast(F32),
                                       b[r * XD:(r + 1) * XD, part, :].bitcast(F32), [tok] + su)
                    hl.used(bk, t2)
                    group["q"][j] = (st, sk, t2)
                return rest
            return mm

        for j in range(2):
            run(xq_piece(j))

        def fill(n, group=group):
            j, i = divmod(n, 2 * GB)
            return [xq_piece(j + 2)] if i == 1 and j + 2 < XPAIRS else []

        units = []
        for j in range(XPAIRS):
            units.append({"heads": 2 * GB, "make": lambda j=j: cross_unit(j, kv, kvk, kv_ok, v_ok, group)})
        attention(units, fill)
        xg_users = []
        t = q.dma(x2_lane, x2[g * GT:(g + 1) * GT, :].rearrange("(a p) n -> p a n", p=P), xg[:, :, :],
                  [group["x_done"]])
        xg_users = [t]
        for m in range(TILES):
            x2_stored[g * TILES + m] = t
    q.phase_end()
    mem.close()

    mem = ExitStack()
    half_tok = TOK // 2
    HB = half_tok // GT
    parts3 = [sb(f"hT3_{n}", [P, KB, GT], F32R, mem) for n in ("hi", "lo")]
    actT = Ring([parts3])
    u1s = [sb(f"u1_{n}", [P, KB, RANK], F32R, mem) for n in ("hi", "lo")]
    v2s = [sb(f"v2_{n}", [P, RB, D], F32R, mem) for n in ("hi", "lo")]
    pT = [sb(f"pT_{n}", [P, RB, TOK], F32R, mem) for n in ("hi", "lo")]
    wraw = Ring([sb(f"w_raw{i}", [P, 3 * RANK], F32, mem) for i in range(3)])
    wsplit = Ring([(sb(f"w_hi{i}", [P, 3 * RANK], F32R, mem), sb(f"w_lo{i}", [P, 3 * RANK], F32R, mem))
                   for i in range(2)])
    gated = Ring([sb(f"gated{i}", [P, GT], F32, mem) for i in range(2)])
    inner = Ring([sb(f"inner{i}", [P, GT], F32, mem) for i in range(2)])
    inner_hl = Ring([sb(f"inner_hl{i}", [P, 2, GT], F32R, mem) for i in range(2)])
    zT = [sb(f"zT_{n}", [P, RB, half_tok], F32R, mem) for n in ("hi", "lo")]
    b1_rows = sb("b1_rows", [2 * FB, P], F32, mem)
    b1c = sb("b1_cols", [P, 2 * FB], F32, mem)
    b2_all = sb("b2_all", [P, D], F32, mem)
    b1_lane, b2_lane = q.lane("b1_loaded"), q.lane("b2_loaded")
    wraw_lanes = [q.lane(f"w_raw{i}_loaded") for i in range(3)]
    out_lanes = [q.lane(f"out_stored{i}") for i in range(3)]

    t = pool(lambda e: e.memset(b1_rows[:, :], 0.0))
    for i in range(2):
        t2 = q.dma(b1_lane, b1_rows[i * FB:i * FB + FB - 1, :],
                   b1[i * INTER:i * INTER + (FB - 1) * P].rearrange("(a b) -> a b", b=P), [t])
        t2 = q.dma(b1_lane, b1_rows[i * FB + FB - 1:i * FB + FB, 0:FLAST],
                   b1[i * INTER + (FB - 1) * P:(i + 1) * INTER].rearrange("(a b) -> a b", a=1), [t])
    J, users, jk = proj.take()
    t = pe(lambda e, J=J: e.transpose(J[:, 0:2 * FB], b1_rows[:, :], ident[0:2 * FB, 0:2 * FB]), [t2] + users, True)
    b1_ok = dve(lambda e, J=J: e.tensor_copy(b1c[:, :], J[:, 0:2 * FB]), [t])
    proj.used(jk, b1_ok)
    b2_ok = q.dma(b2_lane, b2_all[:, :], b2.rearrange("(o n) -> o n", o=1).to_broadcast([P, D]))

    u1_ok, v2_ok = [], []
    for i in range(2):
        buf, k, t = load_into(u1[i * 4 * P:(i + 1) * 4 * P, :].rearrange("(k p) n -> p k n", p=P),
                              lambda b: b[:, :].rearrange("p (k n) -> p k n", k=4))
        ok = split_weight(None, u1s[0][:, 4 * i:4 * i + 4, :], u1s[1][:, 4 * i:4 * i + 4, :],
                          buf[:, :].rearrange("p (k n) -> p k n", k=4), [t])
        xin.used(k, *ok)
        u1_ok += ok
    for i in range(RB):
        buf, k, t = load_into(rows(v2, i), lambda b: b[:, :])
        ok = split_weight(None, v2s[0][:, i, :], v2s[1][:, i, :], buf[:, :], [t])
        xin.used(k, *ok)
        v2_ok += ok

    p_ok = {}

    def rank_down(g):
        parts, ak, ready = turned_group(g, x2, lambda i: [x2_stored[i]], True)
        p_ok[g] = []
        for r in range(RB):
            J, users, jk = proj.take()
            t = down_three(J, users, lambda wp, kb: u1s[wp][:, kb, r * P:(r + 1) * P], parts, ready + u1_ok)
            p_ok[g] += split_bank(J, jk, t, pT[0][:, r, g * GT:(g + 1) * GT], pT[1][:, r, g * GT:(g + 1) * GT], [])
        actT.used(ak, t)

    gate_up = Ring([bank[0], bank[1]] + [bank[2], bank[3]])
    z_banks = [bank[4], bank[5], bank[6], bank[7]]
    def bank_users(ring, k):
        return list(ring.users[k])

    z_users = [[], [], [], []]
    z_ready = []
    zT_users = []

    def inner_weights(f):
        raw, users, k = wraw.take()
        n = P if f < FB - 1 else FLAST
        w = list(users)
        if n < P:
            w.append(pool(lambda e: e.memset(raw[:, :], 0.0), users))
        g4 = raw[:, 0:2 * RANK].rearrange("p (s r n) -> p s r n", s=2, r=RB)
        for s in range(2):
            c = s * INTER + f * P
            t = q.dma(wraw_lanes[k], g4[:, s, :, 0:n], v1[:, c:c + n].rearrange("(r p) n -> p r n", p=P), w)
        t = q.dma(wraw_lanes[k], raw[0:n, 2 * RANK:3 * RANK], u2[f * P:f * P + n, :], w)
        (hi, lo), su, sk = wsplit.take()
        th = pool(lambda e: e.tensor_scalar(hi[:, :], raw[:, :], 1.0, 0.0, ALU.mult, ALU.add), [t] + su)
        tl = pool(lambda e: e.tensor_tensor(lo[:, :], raw[:, :], hi[:, :].bitcast(F32), ALU.subtract), [th] + su)
        wraw.used(k, tl)
        return (hi, lo), sk, [th, tl]

    PASSES = ((0, 0), (0, 1), (1, 0))

    def gate_up_stage(f, g, w, w_ok):
        banks = []
        for s in range(2):
            G, gu, gk = gate_up.take()
            for r in range(RB):
                for n, (wp, ap) in enumerate(PASSES):
                    c = (s * RB + r) * P
                    last = r == RB - 1 and n == 2
                    t = pe(lambda e, G=G, r=r, n=n, wp=wp, ap=ap, c=c, last=last: e.matmul(
                        G[:, :], w[wp][:, c:c + P], pT[ap][:, r, g * GT:(g + 1) * GT],
                        start=r == 0 and n == 0, stop=last), w_ok + p_ok[g] + gu, last)
            banks.append((G, gk, t))
        (G, gk, tg), (U, uk, tu) = banks
        sg, sgu, sgk = gated.take()
        t = act(lambda e: e.activation(sg[:, :], G[:, :], ACT.Silu, bias=b1c[:, f:f + 1]), [tg, b1_ok] + sgu)
        gate_up.used(gk, t)
        a, au, ak = inner.take()
        t = dve(lambda e: e.scalar_tensor_tensor(a[:, :], U[:, :], b1c[:, FB + f:FB + f + 1], sg[:, :],
                                                 ALU.add, ALU.mult), [t, tu] + au)
        gate_up.used(uk, t)
        gated.used(sgk, t)
        b, bu, bk = inner_hl.take()
        th = act(lambda e: e.activation(b[:, 0, :], a[:, :], ACT.Copy), [t] + bu)
        tl = dve(lambda e: e.tensor_tensor(b[:, 1, :], a[:, :], b[:, 0, :].bitcast(F32), ALU.subtract), [th] + bu)
        inner.used(ak, tl)
        return b, bk, [th, tl]

    def z_stage(f, gi, b, bk, b_ok, w, wk_, w_ok, last_use):
        for r in range(RB):
            Z = z_banks[gi * RB + r]
            for n, (wp, ap) in enumerate(PASSES):
                c = 2 * RANK + r * P
                t = pe(lambda e, Z=Z, n=n, wp=wp, ap=ap, c=c: e.matmul(
                    Z[:, :], w[wp][:, c:c + P], b[:, ap, :], start=f == 0 and n == 0, stop=f == FB - 1 and n == 2,
                    skip_group_check=True), b_ok + w_ok + z_users[gi * RB + r], r == RB - 1 and n == 2)
        inner_hl.used(bk, t)
        if last_use:
            wsplit.used(wk_, t)
        return t

    for half in range(2):
        for gi in range(HB):
            rank_down(half * HB + gi)
        everyone = [u for ring in (scores, turned, attn, proj) for us in ring.users for u in us]
        if half == 0:
            for k in range(4):
                gate_up.users[k] += everyone
        for k in range(4):
            z_users[k] = list(everyone)
        steps = [(f, gi) for f in range(FB) for gi in range(HB)]
        loaded = {0: inner_weights(0)}
        pending = []
        for f, gi in steps:
            w, wsk, w_ok = loaded[f]
            b, bk, b_ok = gate_up_stage(f, half * HB + gi, w, w_ok)
            pending.append((f, gi, b, bk, b_ok, w, wsk, w_ok, gi == HB - 1))
            if len(pending) > 1:
                t = z_stage(*pending.pop(0))
            if gi == 0 and f + 1 < FB:
                loaded[f + 1] = inner_weights(f + 1)
        t = z_stage(*pending.pop(0))
        z_ok = []
        for gi in range(HB):
            for r in range(RB):
                Z = z_banks[gi * RB + r]
                hi, lo = (zT[n][:, r, gi * GT:(gi + 1) * GT] for n in range(2))
                th = act(lambda e, Z=Z, hi=hi: e.activation(hi, Z[:, :], ACT.Copy), [t] + zT_users)
                tl = dve(lambda e, Z=Z, hi=hi, lo=lo: e.tensor_tensor(lo, Z[:, :], hi.bitcast(F32), ALU.subtract),
                         [th] + zT_users)
                z_ok += [th, tl]
        for ring in (turned, attn, proj):
            for k in range(len(ring.bufs)):
                ring.used(k, *z_ok)
        for m in range(half_tok // P):
            tile = half * (half_tok // P) + m
            buf, k, loaded_t = load_rows(rows(x2, tile), [x2_stored[tile]])
            tb = pool(lambda e, buf=buf: e.tensor_tensor(buf[:, :], buf[:, :], b2_all[:, :], ALU.add),
                      [loaded_t, b2_ok])
            for n in range(2):
                J, users, jk = proj.take()
                for r in range(RB):
                    for i, (wp, ap) in enumerate(PASSES):
                        last = r == RB - 1 and i == 2
                        t = pe(lambda e, J=J, r=r, i=i, wp=wp, ap=ap, n=n, m=m, last=last: e.matmul(
                            J[:, :], zT[ap][:, r, m * P:(m + 1) * P], v2s[wp][:, r, n * GT:(n + 1) * GT],
                            start=r == 0 and i == 0, stop=last), z_ok + v2_ok + users, last)
                xs = buf[:, n * GT:(n + 1) * GT]
                t2 = dve(lambda e, J=J, xs=xs: e.tensor_tensor(xs, J[:, :], xs, ALU.add), [t, tb])
                proj.used(jk, t2)
            zT_users = [t]
            t3 = q.dma(out_lanes[k], rows(out, tile), buf[:, :], [t2])
            xin.used(k, t3)
    q.phase_end()
    ends = list(q.gate["sync"])
    mem.close()

    with nc.Block() as block:
        @block.sync
        def _(eng):
            q.emit("sync", eng)
            for sem, value in ends:
                eng.wait_ge(sem, value)

        @block.tensor
        def _(eng):
            q.emit("tensor", eng)

        @block.scalar
        def _(eng):
            q.emit("scalar", eng)

        @block.vector
        def _(eng):
            q.emit("vector", eng)

        @block.gpsimd
        def _(eng):
            q.emit("gpsimd", eng)
    ctx.close()


_INS = ["x", "ctx_4096", "L0_attn_q_weight", "L0_attn_q_scale", "L0_attn_k_weight", "L0_attn_k_scale",
        "L0_attn_v_weight", "L0_attn_v_scale", "L0_attn_o_weight", "L0_attn_o_scale", "L0_xattn_Wq_d",
        "L0_xattn_W_qk", "L0_xattn_Wkv_d", "L0_xattn_Wv_u", "L0_ffn_U1", "L0_ffn_V1", "L0_ffn_U2", "L0_ffn_V2",
        "L0_ffn_b1", "L0_ffn_b2"]


def kernel(**inputs):
    import concourse.bacc as bacc
    import numpy as np
    from concourse.bass_utils import run_bass_kernel_spmd

    nc = bacc.Bacc("TRN2", target_bir_lowering=False, num_devices=1)
    arrays, args = {}, []
    for name in _INS:
        a = np.ascontiguousarray(inputs[name])
        if name in ("x", "ctx_4096"):
            a = a.reshape(TOK, D)
        arrays[f"in_{name}"] = a
        args.append(nc.dram_tensor(f"in_{name}", a.shape, mybir.dt.from_np(a.dtype), kind="ExternalInput").ap())
    args.append(nc.dram_tensor("out", (TOK, D), F32, kind="ExternalOutput").ap())
    build_program(nc, *args)
    r = run_bass_kernel_spmd(nc, [arrays], core_ids=[0])
    return r.results[0]["out"].reshape(BATCH, SEQ, D)
```

```python
from contextlib import ExitStack

import concourse.bass as bass
from concourse import mybir

F32 = mybir.dt.float32
F32R = mybir.dt.float32r
F16 = mybir.dt.float16
ALU = mybir.AluOpType
ACT = mybir.ActivationFunctionType
AX = mybir.AxisListType

BATCH, SEQ, D = 8, 256, 1024
P = 128
TOK = BATCH * SEQ
KB = D // P
GT = 512
NG = TOK // GT
TILES = GT // P
GB = GT // SEQ
QT = SEQ // P
HEADS, KV_HEADS = 32, 8
HD = D // HEADS
REP = HEADS // KV_HEADS
KVD = KV_HEADS * HD
XH, XD = 16, 64
XPAIRS = XH // 2
LQ = 128
INTER, RANK = 2752, 256
RB = RANK // P
FB = (INTER + P - 1) // P
FLAST = INTER - (FB - 1) * P
LN_EPS = 1e-5
SIGN_EPS = 1e-8
ON_SCALAR = (1, 4, 6)


class Queues:

    ENGINES = ("tensor", "scalar", "vector", "gpsimd", "sync")

    def __init__(self, nc, ctx):
        self.nc, self.ctx = nc, ctx
        self.queue = {e: [] for e in self.ENGINES}
        self.done = {e: ctx.enter_context(nc.semaphore(f"{e}_done")) for e in self.ENGINES[:4]}
        self.count = {e: 0 for e in self.ENGINES}
        self.gate = {e: [] for e in self.ENGINES}
        self.lanes = []

    def op(self, engine, build, waits=(), signal=True):
        waits = self.gate[engine] + list(waits)
        self.gate[engine] = []
        token = None
        if signal:
            self.count[engine] += 1
            token = (self.done[engine], self.count[engine])
        self.queue[engine].append((waits, build, token and token[0], 1))
        return token

    def lane(self, name):
        lane = [self.ctx.enter_context(self.nc.semaphore(name)), 0]
        self.lanes.append(lane)
        return lane

    def dma(self, lane, out, in_, waits=()):
        waits = self.gate["sync"] + list(waits)
        self.gate["sync"] = []
        lane[1] += 16
        self.queue["sync"].append((waits, lambda e: e.dma_start(out, in_), lane[0], 16))
        return (lane[0], lane[1])

    def phase_end(self):
        last = [(self.done[e], self.count[e]) for e in self.ENGINES[:4] if self.count[e]]
        last += [(lane[0], lane[1]) for lane in self.lanes if lane[1]]
        for e in self.ENGINES:
            self.gate[e] = list(last)

    def emit(self, engine, eng):
        passed = {}
        for waits, build, sem, by in self.queue[engine]:
            for token in waits:
                if token is not None and passed.get(id(token[0]), 0) < token[1]:
                    eng.wait_ge(token[0], token[1])
                    passed[id(token[0])] = token[1]
            ins = build(eng)
            if sem is not None:
                ins.then_inc(sem, by)


class Ring:

    def __init__(self, bufs):
        self.bufs, self.users, self.n = bufs, [[] for _ in bufs], -1

    def take(self):
        self.n += 1
        k = self.n % len(self.bufs)
        assert self.n < len(self.bufs) or self.users[k], "taken before its last user was named"
        users, self.users[k] = self.users[k], []
        return self.bufs[k], users, k

    def used(self, k, *tokens):
        self.users[k] += tokens


def build_program(nc, x, ctx_in, wq, qs, wk, ks, wv, vs, wo, os_, wq_d, w_qk, wkv_d, wv_u,
                  u1, v1, u2, v2, b1, b2, out):
    ctx = ExitStack()
    q = Queues(nc, ctx)
    pe = lambda f, waits=(), signal=False: q.op("tensor", f, waits, signal)
    act = lambda f, waits=(), signal=True: q.op("scalar", f, waits, signal)
    dve = lambda f, waits=(), signal=True: q.op("vector", f, waits, signal)
    pool = lambda f, waits=(), signal=True: q.op("gpsimd", f, waits, signal)

    def sb(name, shape, dt, where=ctx):
        return where.enter_context(nc.sbuf_tensor(name, shape, dt))

    x1 = nc.dram_tensor("x1_scratch", [TOK, D], F32, kind="Internal").ap()
    x2 = nc.dram_tensor("x2_scratch", [TOK, D], F32, kind="Internal").ap()
    rows = lambda a, tile: a[tile * P:(tile + 1) * P, :]

    ident = sb("ident", [P, P], F32)
    ident16 = sb("ident16", [P, P], F16)
    ones = sb("ones", [P, P], F32)
    neg_half = sb("neg_half", [P, 1], F32)
    xin_bufs = [sb(f"xin{i}", [P, D], F32) for i in range(3)]
    prob = Ring([sb(f"prob{i}", [P, GT], F32) for i in range(3)])
    probT = Ring([sb(f"probT{i}", [P, GT], F32) for i in range(6)])
    tmp = Ring([sb(f"tmp{i}", [P, GT], F32) for i in range(2)])
    xin = Ring(xin_bufs)
    xin_lane = [q.lane(f"xin{i}_loaded") for i in range(3)]
    bn = Ring([sb(f"bn{i}", [P, 16], F32) for i in range(4)])
    maxes = Ring([sb(f"maxes{i}", [P, 4], F32) for i in range(4)])
    row_sums = Ring([sb(f"row_sums{i}", [P, 4, REP], F32) for i in range(3)])

    bank = [ctx.enter_context(nc.psum_tensor(f"bank{i}", [P, GT], F32)) for i in range(8)]
    scores = Ring(bank[0:3])
    turned = Ring(bank[3:5])
    attn = Ring(bank[5:6])
    proj = Ring(bank[6:8])

    c0 = pool(lambda e: e.memset(ident[:, :], 0.0))
    c1 = pool(lambda e: e.affine_select(out=ident[:, :], in_=ident[:, :], compare_op=ALU.not_equal, fill=1.0,
                                        base=0, pattern=[[-1, P]], channel_multiplier=1), [c0])
    ident_ok = pool(lambda e: e.tensor_copy(ident16[:, :], ident[:, :]), [c1])
    ones_ok = pool(lambda e: e.memset(ones[:, :], 1.0))
    half_ok = pool(lambda e: e.memset(neg_half[:, :], -0.5))

    def load_rows(src, waits=()):
        buf, users, k = xin.take()
        return buf, k, q.dma(xin_lane[k], buf[:, :], src, list(users) + list(waits))

    def layernorm(buf, k, loaded):
        st, users, sk = bn.take()
        t = [dve(lambda e, i=i: e.bn_stats(st[:, 6 * i:6 * i + 6], buf[:, GT * i:GT * (i + 1)]),
                 [loaded] + users) for i in range(2)]
        t = dve(lambda e: e.bn_aggr(st[:, 12:14], st[:, 0:12]), t)
        dve(lambda e: e.tensor_scalar(st[:, 12:13], st[:, 12:13], -1.0, None, ALU.mult), [t], False)
        t = dve(lambda e: e.tensor_scalar(st[:, 14:15], st[:, 13:14], LN_EPS, None, ALU.add), [t])
        t = pool(lambda e: e.tensor_tensor(st[:, 15:16], st[:, 14:15], neg_half[:, :], ALU.pow), [t, half_ok])
        t = pool(lambda e: e.tensor_scalar(buf[:, :], buf[:, :], st[:, 12:13], st[:, 15:16], ALU.add, ALU.mult), [t])
        bn.used(sk, t)
        return t

    def transpose_tile(src, ready, hi, lo, m, waits, used):
        pieces = []
        for half in range(2):
            def mm(half=half):
                J, users, jk = proj.take()
                for i in range(4):
                    kb = 4 * half + i
                    t = pe(lambda e, i=i, kb=kb: e.transpose(J[:, i * P:(i + 1) * P], src[:, kb * P:(kb + 1) * P],
                                                             ident[:, :]),
                           [ready, ident_ok] + users, signal=i == 3)
                used(t)

                def split():
                    J3 = J[:, :].rearrange("p (k n) -> p k n", k=4)
                    dst = lambda a: a[:, 4 * half:4 * half + 4, m * P:(m + 1) * P]
                    th = act(lambda e: e.activation(dst(hi), J3, ACT.Copy), [t] + waits)
                    tl = dve(lambda e: e.tensor_tensor(dst(lo), J3, as_f32(dst(hi)), ALU.subtract), [th] + waits)
                    proj.used(jk, tl)
                    return [th, tl]
                return split
            pieces.append(mm)
        return pieces

    def as_f32(a):
        return a.bitcast(F32) if a.dtype == F32R else a

    def run(piece):
        rest = piece()
        return rest() if rest else None

    def score_stage(mms, scale):
        S, users, sk = scores.take()
        t = mms(S, users)
        mx, mu, mk = maxes.take()
        S3 = S[:, :].rearrange("p (a b) -> p a b", a=QT)
        t = dve(lambda e: e.tensor_reduce(mx[:, 0:QT], S3, AX.X, ALU.max), [t] + mu)
        t = dve(lambda e: e.tensor_scalar(mx[:, QT:2 * QT], mx[:, 0:QT], -scale, None, ALU.mult), [t])
        return S, sk, mx, mk, t

    def exp_stage(S, sk, mx, mk, t, scale, sums):
        Pb, pu, pk = prob.take()
        te = [act(lambda e, a=a, total=sums(a): e.activation(
                      Pb[:, a * SEQ:(a + 1) * SEQ], S[:, a * SEQ:(a + 1) * SEQ], ACT.Exp,
                      bias=mx[:, QT + a:QT + a + 1], scale=scale, accum_out=total),
                  [t] + pu) for a in range(QT)]
        scores.used(sk, te[-1])
        maxes.used(mk, te[-1])
        return Pb, pk, te

    def turn_stage(Pb, pk, te):
        T, users, tk = turned.take()
        for kt in range(QT):
            for qt in range(QT):
                t = pe(lambda e, kt=kt, qt=qt: e.transpose(
                    T[:, kt * SEQ + qt * P:kt * SEQ + (qt + 1) * P],
                    Pb[:, qt * SEQ + kt * P:qt * SEQ + (kt + 1) * P], ident[:, :]),
                    te + users, signal=kt == QT - 1 and qt == QT - 1)
        prob.used(pk, t)
        return T, tk, t

    def evac_stage(T, tk, t, n):
        PT, ptu, ptk = probT.take()
        if n % 8 in ON_SCALAR:
            t = act(lambda e: e.activation(PT[:, :], T[:, :], ACT.Copy), [t] + ptu)
        else:
            t = dve(lambda e: e.tensor_copy(PT[:, :], T[:, :]), [t] + ptu)
        turned.used(tk, t)
        return PT, ptk, t

    AHEAD = 3

    def attention(units, side_work):
        heads = [(u, i) for u in units for i in range(u["heads"])]
        scored, soft, ready, rest = {}, {}, {}, []

        def score(n):
            if n < len(heads):
                u, i = heads[n]
                if i == 0:
                    u.update(u.pop("make")())
                    u["begin"]()
                scored[n] = score_stage(lambda S, w: u["scores"](i, S, w), u["scale"])

        def exp(n):
            if n < len(heads):
                u, i = heads[n]
                soft[n] = exp_stage(*scored.pop(n), u["scale"], lambda a: u["sums"](i, a))
                u["box"]["exp"] = soft[n][2][-1]

        for n in range(AHEAD):
            score(n)
        exp(0)
        finish = []
        for n in range(len(heads) + 1):
            score(n + AHEAD)
            if n < len(heads):
                T = turn_stage(*soft.pop(n))
                exp(n + 1)
                ready[n] = evac_stage(*T, n)
            for r in rest:
                r()
            rest = []
            for piece in side_work(n):
                r = piece()
                if r:
                    rest.append(r)
            if finish:
                finish.pop(0)()
            if n >= 1:
                u, i = heads[n - 1]
                s = u["set"]
                if i % s == s - 1:
                    u["values"](i // s, [ready.pop(n - s + j) for j in range(s)])
                if i == u["heads"] - 1:
                    finish += u["end"]()
        return rest + finish

    mem = ExitStack()
    sW = sb("signs_qkv", [P, KB, D + 2 * KVD], F16, mem)
    sWo = sb("signs_o", [P, KB, D], F32R, mem)
    NSC = (2 * D + 2 * KVD) // P
    QB, VB, OB = KB, KB + KVD // P, KB + 2 * KVD // P
    sc_rows = sb("scale_rows", [NSC, P], F32, mem)
    sc = sb("scale_cols", [P, NSC], F32, mem)
    abs_sum = sb("abs_sum", [P, NSC], F32, mem)
    s_mean = sb("s_mean", [P, NSC], F32, mem)
    chan = sb("channel_scale", [P, NSC], F32, mem)
    cv = sb("v_scale_all", [P, KVD], F32, mem)
    co = sb("o_scale_all", [P, D], F32, mem)
    sign_ring = Ring([sb(f"sign{i}", [P, D], F16, mem) for i in range(2)])
    hT_hi = sb("hT_hi", [P, KB, GT], F16, mem)
    hT_lo = sb("hT_lo", [P, KB, GT], F16, mem)
    kst = sb("k_stack", [P, KV_HEADS, GT], F32R, mem)
    vall = sb("v_all", [P, TILES, KVD], F32, mem)
    hl = Ring([sb(f"hi_lo{i}", [P, 2, GT], F32R, mem) for i in range(2)])
    qst = Ring([sb(f"q_stack{i}", [P, REP, GT], F32R, mem) for i in range(2)])
    OT_hi = sb("attnT_hi", [P, KB, GT], F32R, mem)
    OT_lo = sb("attnT_lo", [P, KB, GT], F32R, mem)
    r_all = sb("recip_all", [P, 4, REP, HD], F32, mem)
    R_sb = sb("recipT", [P, GT], F32, mem)
    OTn = sb("attnT", [P, GT], F32, mem)
    xres = Ring([sb(f"x_res{i}", [P, D], F32, mem) for i in range(2)])
    sc_lane = q.lane("scales_loaded")
    st_lanes = [q.lane(f"stack{i}_loaded") for i in range(2)]
    k_lanes = [q.lane(f"k_stack{i}_loaded") for i in range(2)]
    xres_lanes = [q.lane(f"x_res{i}_loaded") for i in range(2)]
    x1_lanes = [q.lane(f"x1_stored{i}") for i in range(2)]

    zeroed = [pool(lambda e, a=a: e.memset(a[:, :, :].bitcast(F32), 0.0)) for a in [kst] + qst.bufs]

    t = None
    for src, n, at in ((qs, KB, 0), (ks, KVD // P, QB), (vs, KVD // P, VB), (os_, KB, OB)):
        t = q.dma(sc_lane, sc_rows[at:at + n, :], src.rearrange("(a b) -> a b", b=P))
    J, users, jk = proj.take()
    t = pe(lambda e: e.transpose(J[:, 0:NSC], sc_rows[:, :], ident[0:NSC, 0:NSC]), [t, ident_ok], True)
    sc_ok = dve(lambda e: e.tensor_copy(sc[:, :], J[:, 0:NSC]), [t])
    proj.used(jk, sc_ok)

    chan_ok = {}
    signs_ok = {}

    def sign_pieces(src, tile, idx, dst, at):
        box = {}
        c = slice(idx, idx + 1)

        def load():
            box["w"], box["k"], box["loaded"] = load_rows(rows(src, tile))

        def mean():
            sg, sgu, box["sk"] = sign_ring.take()
            box["sg"] = sg
            t = act(lambda e: e.activation(sg[:, :], box["w"][:, :], ACT.Abs, accum_out=abs_sum[:, c]),
                    [box["loaded"]] + sgu)
            box["abs"] = t
            t = dve(lambda e: e.tensor_scalar(s_mean[:, c], abs_sum[:, c], 1.0 / D, SIGN_EPS, ALU.mult, ALU.max), [t])
            chan_ok[idx] = dve(lambda e: e.tensor_tensor(chan[:, c], s_mean[:, c], sc[:, c], ALU.mult), [t, sc_ok])

        def sign():
            t = act(lambda e: e.activation(box["sg"][:, :], box["w"][:, :], ACT.Sign), [box["abs"]])
            box["t"] = t
            xin.used(box["k"], t)

        def mm():
            J, users, jk = proj.take()
            J16 = J[:, :].bitcast(F16)
            for kb in range(KB):
                tt = pe(lambda e, kb=kb: e.transpose(J16[:, kb * P:(kb + 1) * P], box["sg"][:, kb * P:(kb + 1) * P],
                                                     ident16[:, :]), [box["t"], ident_ok] + users, kb == KB - 1)
            sign_ring.used(box["sk"], tt)

            def evac():
                J3 = J16.rearrange("p (k n) -> p k n", k=KB)
                signs_ok[idx] = dve(lambda e: e.tensor_copy(dst[:, :, at:at + P], J3), [tt])
                proj.used(jk, signs_ok[idx])
            return evac
        return load, mean, sign, mm

    def scale_all(first, n, dst):
        last = None
        for half in range((n + 3) // 4):
            J, users, jk = proj.take()
            m = min(4, n - 4 * half)
            for i in range(m):
                idx = first + 4 * half + i
                dg, du, dk = tmp.take()
                t = dve(lambda e, idx=idx, dg=dg: e.tensor_scalar(dg[:, 0:P], ident[:, :], chan[:, idx:idx + 1], None,
                                                                  ALU.mult), [chan_ok[idx], ident_ok] + du)
                t = pe(lambda e, i=i, dg=dg, J=J: e.matmul(J[:, i * P:(i + 1) * P], ones[:, :], dg[:, 0:P],
                                                           start=True, stop=True), [t, ones_ok] + users, True)
                tmp.used(dk, t)
            last = dve(lambda e, half=half, m=m, J=J: e.tensor_copy(dst[:, half * GT:half * GT + m * P],
                                                                    J[:, 0:m * P]), [t])
            proj.used(jk, last)
        return last

    hT_users = []
    hT_ready = []
    kst_users, v_users, OT_users = [], [], []

    def ln_pieces(g):
        preps, turns, shared = [], [], {}
        for m in range(TILES):
            box = {}

            def prep(m=m, box=box):
                buf, k, loaded = load_rows(rows(x, g * TILES + m))
                box["tile"] = buf, k, layernorm(buf, k, loaded)

            def turn(half, m=m, box=box):
                if m == 0 and half == 0:
                    shared["users"] = list(hT_users)
                    hT_users.clear()
                    hT_ready.clear()
                if half == 0:
                    buf, k, ok = box["tile"]
                    box["p"] = transpose_tile(buf, ok, hT_hi, hT_lo, m, shared["users"], lambda t: xin.used(k, t))
                r = box["p"][half]()
                return lambda: hT_ready.extend(r())
            preps.append(prep)
            turns.append([lambda turn=turn, half=half: turn(half) for half in range(2)])
        return preps, turns

    def split_scaled(J, jk, t, idx):
        b, bu, bk = hl.take()
        c = chan[:, idx:idx + 1]
        th = act(lambda e: e.activation(b[:, 0, :], J[:, :], ACT.Copy, scale=c), [t, chan_ok[idx]] + bu)
        tl = dve(lambda e: e.scalar_tensor_tensor(b[:, 1, :], J[:, :], c, b[:, 0, :].bitcast(F32),
                                                  ALU.mult, ALU.subtract), [th, chan_ok[idx]] + bu)
        proj.used(jk, tl)
        return b, bk, th, tl

    kst_ready = {}

    def k_piece(kt):
        def mm():
            J, users, jk = proj.take()
            for kb in range(KB):
                for part in (hT_hi, hT_lo):
                    last = kb == KB - 1 and part is hT_lo
                    t = pe(lambda e, kb=kb, part=part, last=last: e.matmul(
                        J[:, :], sW[:, kb, D + kt * P:D + (kt + 1) * P], part[:, kb, :],
                        start=kb == 0 and part is hT_hi, stop=last), hT_ready + users + [signs_ok[QB + kt]], last)
            hT_users.append(t)

            def rest():
                b, bk, th, tl = split_scaled(J, jk, t, QB + kt)
                lane = k_lanes[kt]
                for part, tok, at in ((0, th, (0, 1)), (1, tl, (2,))):
                    for a in at:
                        for i in range(P // HD):
                            t2 = q.dma(lane, kst[a * HD:(a + 1) * HD, kt * (P // HD) + i, :].bitcast(F32),
                                       b[i * HD:(i + 1) * HD, part, :].bitcast(F32), [tok] + kst_users + zeroed)
                hl.used(bk, t2)
                kst_ready[kt] = t2
            return rest
        return mm

    v_ready = []

    def v_piece(pair):
        def mm():
            J, users, jk = proj.take()
            for i in range(2):
                m = 2 * pair + i
                for kb in range(KB):
                    for part in (hT_hi, hT_lo):
                        last = kb == KB - 1 and part is hT_lo
                        t = pe(lambda e, i=i, m=m, kb=kb, part=part, last=last: e.matmul(
                            J[:, i * KVD:(i + 1) * KVD], part[:, kb, m * P:(m + 1) * P], sW[:, kb, D + KVD:D + 2 * KVD],
                            start=kb == 0 and part is hT_hi, stop=last),
                            hT_ready + users + [signs_ok[VB], signs_ok[VB + 1]], last and i == 1)
            hT_users.append(t)

            def rest():
                cvb = cv[:, :].rearrange("p (o n) -> p o n", o=1).to_broadcast([P, 2, KVD])
                t2 = dve(lambda e: e.tensor_tensor(vall[:, 2 * pair:2 * pair + 2, :],
                                                   J[:, :].rearrange("p (o n) -> p o n", o=2), cvb, ALU.mult),
                         [t, cv_ok[0]] + v_users)
                proj.used(jk, t2)
                v_ready.append(t2)
            return rest
        return mm

    q_ready = {}

    def q_pieces(g, tq, n_chunks=4):
        box = {}

        def chunk(c):
            if c == 0:
                box["J"] = proj.take()
            J, users, jk = box["J"]
            for kb in range(c * KB // n_chunks, (c + 1) * KB // n_chunks):
                for part in (hT_hi, hT_lo):
                    last = kb == KB - 1 and part is hT_lo
                    t = pe(lambda e, kb=kb, part=part, last=last: e.matmul(
                        J[:, :], sW[:, kb, tq * P:(tq + 1) * P], part[:, kb, :],
                        start=kb == 0 and part is hT_hi, stop=last), hT_ready + users + [signs_ok[tq]], last)
            if c < n_chunks - 1:
                return None
            hT_users.append(t)

            def rest():
                b, bk, th, tl = split_scaled(J, jk, t, tq)
                st, su, sk = qst.take()
                lane = st_lanes[sk]
                for part, tok, at in ((0, th, (0, 2)), (1, tl, (1,))):
                    for a in at:
                        for i in range(REP):
                            t2 = q.dma(lane, st[a * HD:(a + 1) * HD, i, :].bitcast(F32),
                                       b[i * HD:(i + 1) * HD, part, :].bitcast(F32), [tok] + su + zeroed)
                hl.used(bk, t2)
                q_ready[g, tq] = (st, sk, t2)
            return rest
        return [lambda c=c: chunk(c) for c in range(n_chunks)]

    OT_ready = {}

    def self_unit(g, tq):
        u = {"heads": GB * REP, "scale": HD ** -0.5, "set": REP}
        box = {}

        def begin():
            box["q"] = q_ready[g, tq]
            box["sums"], box["su"], box["sk"] = row_sums.take()

        def mk_scores(i, S, waits):
            b, r = divmod(i, REP)
            st, sk, ready = box["q"]
            for a in range(QT):
                t = pe(lambda e, a=a: e.matmul(S[:, a * SEQ:(a + 1) * SEQ],
                                               st[:, r, b * SEQ + a * P:b * SEQ + (a + 1) * P],
                                               kst[:, tq, b * SEQ:(b + 1) * SEQ], start=True, stop=True),
                       waits + zeroed + [ready, kst_ready[tq // (P // HD)]] + box["su"], a == QT - 1)
            if i == GB * REP - 1:
                qst.used(sk, t)
                kst_users.append(t)
            return t

        def sums(i, a):
            b, r = divmod(i, REP)
            return box["sums"][:, b * QT + a, r:r + 1]

        def values(b, pts):
            if b == 0:
                box["O"], box["ou"], box["ok"] = attn.take()
            O = box["O"]
            for kt in range(QT):
                for r in range(REP):
                    PT, ptk, tp = pts[r]
                    t = pe(lambda e, kt=kt, r=r, PT=PT: e.matmul(
                        O[r * HD:(r + 1) * HD, b * SEQ:(b + 1) * SEQ], vall[:, b * QT + kt, tq * HD:(tq + 1) * HD],
                        PT[:, kt * SEQ:(kt + 1) * SEQ], start=kt == 0, stop=kt == QT - 1,
                        tile_position=(0, r * HD)), [tp] + v_ready + box["ou"], kt == QT - 1)
                    if kt == QT - 1:
                        probT.used(ptk, t)
            box["o_t"] = t

        def end():
            s = box["sums"]
            t = dve(lambda e: e.reciprocal(s[:, :, :], s[:, :, :]), [box["exp"]])
            t = pool(lambda e: e.tensor_scalar(
                r_all[:, :, :, :].rearrange("p a r d -> p (a r) d"),
                s[:, :, :].rearrange("p a (r o) -> p (a r) o", o=1).to_broadcast([P, 4 * REP, HD]),
                1.0, 0.0, ALU.mult, ALU.add), [t] + r_users)
            r_users.clear()
            row_sums.used(box["sk"], t)
            return [lambda: finish(t)]

        def finish(t):
            J, users, jk = proj.take()
            for a in range(4):
                t2 = pe(lambda e, a=a: e.transpose(J[:, a * P:(a + 1) * P],
                                                   r_all[:, a, :, :].rearrange("p r d -> p (r d)"), ident[:, :]),
                        [t] + users, a == 3)
            r_users.append(t2)
            t3 = act(lambda e: e.activation(R_sb[:, :], J[:, :], ACT.Copy), [t2] + R_users)
            proj.used(jk, t3)
            t4 = dve(lambda e: e.tensor_tensor(OTn[:, :], box["O"][:, :], R_sb[:, :], ALU.mult),
                     [t3, box["o_t"]] + OTn_users)
            R_users[:] = [t4]
            attn.used(box["ok"], t4)
            t5 = pool(lambda e: e.tensor_scalar(OT_hi[:, tq, :], OTn[:, :], 1.0, 0.0, ALU.mult, ALU.add),
                      [t4] + OT_users)
            t6 = pool(lambda e: e.tensor_tensor(OT_lo[:, tq, :], OTn[:, :], OT_hi[:, tq, :].bitcast(F32),
                                                ALU.subtract), [t5] + OT_users)
            OTn_users[:] = [t6]
            OT_ready[tq] = t6
            if tq == KV_HEADS - 1:
                v_users.clear()
                v_users.append(box["o_t"])
        u.update(begin=begin, scores=mk_scores, sums=sums, values=values, end=end, box=box)
        return u

    r_users, R_users, OTn_users = [], [], []

    def o_pieces(g):
        pieces, loads = [], []
        ready = {}
        for m in range(TILES):
            box = {}

            def load(m=m, box=box):
                box["x"], users, box["k"] = xres.take()
                box["xl"] = q.dma(xres_lanes[box["k"]], box["x"][:, :], rows(x, g * TILES + m), users)
            loads.append(load)
            for n in range(2):
                def mm(m=m, n=n, box=box):
                    if not ready:
                        ready.update(OT_ready)
                        OT_ready.clear()
                    J, users, jk = proj.take()
                    for tq in range(KB):
                        for part in (OT_hi, OT_lo):
                            last = tq == KB - 1 and part is OT_lo
                            t = pe(lambda e, tq=tq, part=part, last=last: e.matmul(
                                J[:, :], part[:, tq, m * P:(m + 1) * P], sWo[:, tq, n * GT:(n + 1) * GT],
                                start=tq == 0 and part is OT_hi, stop=last),
                                [ready[tq]] + users + [signs_ok[OB + i] for i in range(KB)], last)
                    if m == TILES - 1 and n == 1:
                        OT_users[:] = [t]

                    def rest():
                        y, yu, yk = tmp.take()
                        xs = box["x"][:, n * GT:(n + 1) * GT]
                        t2 = dve(lambda e: e.tensor_tensor(y[:, :], J[:, :], co[:, n * GT:(n + 1) * GT], ALU.mult),
                                 [t, co_ok[0]] + yu)
                        proj.used(jk, t2)
                        t3 = pool(lambda e: e.tensor_tensor(xs, xs, y[:, :], ALU.add), [t2, box["xl"]])
                        tmp.used(yk, t3)
                        if n == 1:
                            t4 = q.dma(x1_lanes[box["k"]], rows(x1, g * TILES + m), box["x"][:, :], [t3])
                            xres.used(box["k"], t4)
                            x1_stored[g * TILES + m] = t4
                    return rest
                pieces.append(mm)
        return loads, pieces

    x1_stored = {}
    cv_ok, co_ok = [None], [None]

    signs_q = [sign_pieces(wq, i, i, sW, i * P) for i in range(KB)]
    signs_o = [sign_pieces(wo, i, OB + i, sWo, i * P) for i in range(KB)]
    first_signs = [sign_pieces(wk, i, QB + i, sW, D + i * P) for i in range(KVD // P)]
    first_signs += [signs_q[0]]
    first_signs += [sign_pieces(wv, i, VB + i, sW, D + KVD + i * P) for i in range(KVD // P)]
    first_signs += signs_q[1:3]
    preps, turns = ln_pieces(0)
    work = []
    for m in range(TILES):
        work += [(first_signs[m][0], preps[m]), (first_signs[m][1], first_signs[m][2], first_signs[m][3]),
                 tuple(turns[m])]
    for s in first_signs[TILES:]:
        work.append(s)
    for group in work:
        for piece in group:
            run(piece)
    cv_ok[0] = scale_all(VB, KVD // P, cv)

    def kvq_pieces(g):
        def whole(pieces):
            def mm():
                rest = None
                for p in pieces:
                    rest = p() or rest
                return rest
            return mm
        return {"k": [k_piece(kt) for kt in range(KVD // P)], "v": [v_piece(i) for i in range(TILES // 2)],
                "q": [whole(q_pieces(g, tq)) for tq in range(2)]}

    new = kvq_pieces(0)
    for piece in (new["k"][0], new["q"][0], new["v"][0], new["v"][1], new["q"][1], new["k"][1]):
        run(piece)
    o_loads, o_left = [], []
    for g in range(NG):
        units = [{"heads": GB * REP, "make": lambda tq=tq, g=g: self_unit(g, tq)} for tq in range(KV_HEADS)]
        queries = {}
        plan = {}
        if o_left:
            plan[0, 0], plan[0, 1] = [o_left[0]], [o_left[1]]
        for u in range(KV_HEADS - 2):
            for i in range(4):
                def chunk(u=u, i=i, g=g, queries=queries):
                    if i == 0:
                        queries[u] = q_pieces(g, u + 2)
                    return queries[u][i]()
                plan.setdefault((u, i + 2), []).append(chunk)
        if g == 0:
            for u in range(KV_HEADS):
                turns_at = [(signs_o[u], (3, 4, 5, 7) if u + 3 < KB else (0, 1, 2, 4))]
                if u + 3 < KB:
                    turns_at.append((signs_q[u + 3], (0, 1, 2, 4)))
                for pieces, at in turns_at:
                    for piece, i in zip(pieces, at):
                        plan.setdefault((u, i), []).append(piece)
        o_loads, o_work = o_pieces(g)
        last = KV_HEADS - 1
        plan.setdefault((last, 5), []).append(o_loads[0])
        plan.setdefault((last, 7), []).append(o_loads[1])
        if g + 1 < NG:
            preps, turns = ln_pieces(g + 1)
            plan.setdefault((last, 2), []).append(preps[0])
            plan.setdefault((last, 6), []).append(preps[1])
        late = attention(units, lambda n: plan.get(divmod(n, GB * REP), []))
        if g == 0:
            co_ok[0] = scale_all(OB, KB, co)
        if g + 1 < NG:
            v_ready.clear()
            new = kvq_pieces(g + 1)
            kst_clear = lambda: kst_users.clear()
            order = [preps[2], turns[0][0], turns[0][1], *late, preps[3], turns[1][0], turns[1][1], o_work[0], turns[2][0],
                     turns[2][1], o_work[1], o_loads[2], turns[3][0], turns[3][1], o_work[2], new["k"][0],
                     new["q"][0], o_work[3], o_loads[3], new["v"][0], new["v"][1], o_work[4], new["k"][1],
                     kst_clear, new["q"][1], o_work[5]]
            o_left = o_work[6:]
            for piece in order:
                run(piece)
        else:
            for f in late:
                f()
            for i, piece in enumerate(o_work):
                run(piece)
                if i in (1, 3):
                    o_loads[i // 2 + 2]()
    q.phase_end()
    mem.close()

    mem = ExitStack()
    actT = Ring([(sb(f"actT_hi{i}", [P, KB, GT], F32R, mem), sb(f"actT_lo{i}", [P, KB, GT], F32R, mem))
                 for i in range(2)])
    wqd = [sb(f"wq_down_{n}", [P, KB, LQ], F32R, mem) for n in ("hi", "lo")]
    wqk = [sb(f"w_qk_{n}", [P, XH * XD], F32R, mem) for n in ("hi", "lo")]
    wkv = [sb(f"wkv_down_{n}", [P, KB, 2, XD], F32R, mem) for n in ("hi", "lo")]
    wvu = sb("wv_up", [P, XH * XD], F32R, mem)
    cq = sb("cq_hi_lo", [P, 2, GT], F32R, mem)
    ckv = Ring([sb(f"ckv{i}", [P, 2, GT], F32R, mem) for i in range(2)])
    xv = sb("xv_all", [P, TILES, XH * XD], F32, mem)
    hl = Ring([sb(f"xhi_lo{i}", [P, 2, GT], F32R, mem) for i in range(2)])
    xst = Ring([sb(f"xq_stack{i}", [P, 2, GT], F32R, mem) for i in range(3)])
    xg = sb("x_group", [P, TILES, D], F32, mem)
    OTs = Ring([sb(f"xattnT{i}", [P, GT], F32, mem) for i in range(2)])
    xr = Ring([sb(f"xrecip{i}", [P, 4, 2], F32, mem) for i in range(2)])
    xst_lanes = [q.lane(f"xq_stack{i}_loaded") for i in range(3)]
    xg_lanes = [q.lane(f"x_group{j}_loaded") for j in range(XPAIRS)]
    x2_lanes = [q.lane(f"x2_stored{j}") for j in range(XPAIRS)]

    def split_weight(hi, lo, shape_view, waits):
        th = pool(lambda e: e.tensor_scalar(hi, shape_view, 1.0, 0.0, ALU.mult, ALU.add), waits)
        tl = dve(lambda e: e.tensor_tensor(lo, shape_view, hi.bitcast(F32), ALU.subtract), [th])
        return [th, tl]

    def load_into(src, view, waits=()):
        buf, users, k = xin.take()
        return buf, k, q.dma(xin_lane[k], view(buf), src, list(users) + list(waits))

    buf, k, t = load_into(wq_d.rearrange("(k p) n -> p k n", p=P),
                          lambda b: b[:, :].rearrange("p (k n) -> p k n", k=KB))
    wqd_ok = split_weight(wqd[0][:, :, :], wqd[1][:, :, :], buf[:, :].rearrange("p (k n) -> p k n", k=KB), [t])
    xin.used(k, *wqd_ok)
    buf, k, t = load_into(w_qk, lambda b: b[:, :])
    wqk_ok = split_weight(wqk[0][:, :], wqk[1][:, :], buf[:, :], [t])
    xin.used(k, *wqk_ok)
    buf, k, t = load_into(wkv_d.rearrange("(k p) n -> p k n", p=P),
                          lambda b: b[:, 0:KB * XD].rearrange("p (k n) -> p k n", k=KB))
    view = buf[:, 0:KB * XD].rearrange("p (k n) -> p k n", k=KB)
    wkv_ok = []
    for c in range(2):
        wkv_ok += split_weight(wkv[0][:, :, c, :], wkv[1][:, :, c, :], view, [t])
    xin.used(k, *wkv_ok)
    buf, k, t = load_into(wv_u, lambda b: b[0:XD, :])
    t2 = q.dma(xin_lane[k], buf[XD:P, :], wv_u)
    t = pool(lambda e, buf=buf: e.tensor_scalar(wvu[:, :], buf[:, :], 1.0, 0.0, ALU.mult, ALU.add), [t, t2])
    wvu_ok = dve(lambda e, buf=buf: e.tensor_tensor(wvu[XD:P, :], buf[XD:P, :], wvu[XD:P, :].bitcast(F32),
                                                    ALU.subtract), [t])
    xin.used(k, wvu_ok)

    def split_bank(J, jk, t, hi, lo, waits):
        th = act(lambda e: e.activation(hi, J[:, :], ACT.Copy), [t] + waits)
        tl = dve(lambda e: e.tensor_tensor(lo, J[:, :], hi.bitcast(F32), ALU.subtract), [th] + waits)
        proj.used(jk, tl)
        return [th, tl]

    def down_three(J, users, w, parts, ready):
        n = 0
        for kb in range(KB):
            for wp, ap in ((0, 0), (0, 1), (1, 0)):
                last = kb == KB - 1 and wp == 1
                t = pe(lambda e, kb=kb, wk=w(wp, kb), ap=ap, first=n == 0, last=last: e.matmul(
                    J[:, :], wk, parts[ap][:, kb, :], start=first, stop=last), ready + users, last)
                n += 1
        return t

    def turned_group(g, src, waits, normed):
        state, preps, turns = {"ready": []}, [], []
        for m in range(TILES):
            def prep(m=m):
                buf, k, loaded = load_rows(rows(src, g * TILES + m), waits)
                state[m] = buf, k, (layernorm(buf, k, loaded) if normed else loaded)

            def turn(half, m=m):
                if m == 0 and half == 0:
                    state["parts"], state["users"], state["k"] = actT.take()
                if half == 0:
                    buf, k, ok = state[m]
                    state["p"] = transpose_tile(buf, ok, state["parts"][0], state["parts"][1], m, state["users"],
                                                lambda t: xin.used(k, t))
                r = state["p"][half]()
                return lambda: state["ready"].extend(r())
            preps.append(prep)
            turns += [lambda turn=turn, half=half: turn(half) for half in range(2)]
        return state, preps, turns

    cq_users, xv_users = [], []
    x2_stored = []
    cols = lambda a, g, j: a[g * GT:(g + 1) * GT, j * P:(j + 1) * P].rearrange("(a p) n -> p a n", p=P)
    xg_loaded = {j: q.dma(xg_lanes[j], xg[:, :, j * P:(j + 1) * P], cols(x1, 0, j), list(x1_stored.values()))
                 for j in range(XPAIRS)}

    def cross_unit(g, j, kv, kvk, kv_ok, v_ok, stacks, n_heads=2 * GB):
        box = {}
        st, sk, ready = stacks[j]

        def begin():
            box["sums"], box["su"], box["sk"] = row_sums.take()

        def mk_scores(i, S, waits):
            b, r = divmod(i, 2)
            for a in range(QT):
                for part in range(2):
                    t = pe(lambda e, a=a, part=part: e.matmul(
                        S[:, a * SEQ:(a + 1) * SEQ], st[:, r, b * SEQ + a * P:b * SEQ + (a + 1) * P],
                        kv[:, part, b * SEQ:(b + 1) * SEQ], start=part == 0, stop=part == 1),
                        waits + [ready] + kv_ok + box["su"], a == QT - 1 and part == 1)
            if i == n_heads - 1:
                xst.used(sk, t)
                if j == XPAIRS - 1:
                    ckv.used(kvk, t)
            return t

        def sums(i, a):
            b, r = divmod(i, 2)
            return box["sums"][:, b * QT + a, r:r + 1]

        def values(b, pts):
            if b == 0:
                box["O"], box["ou"], box["ok"] = attn.take()
            O = box["O"]
            for kt in range(QT):
                for r in range(2):
                    PT, ptk, tp = pts[r]
                    t = pe(lambda e, kt=kt, r=r, PT=PT: e.matmul(
                        O[r * XD:(r + 1) * XD, b * SEQ:(b + 1) * SEQ],
                        xv[:, b * QT + kt, (2 * j + r) * XD:(2 * j + r + 1) * XD],
                        PT[:, kt * SEQ:(kt + 1) * SEQ], start=kt == 0, stop=kt == QT - 1,
                        tile_position=(0, r * XD)), [tp] + v_ok + box["ou"], kt == QT - 1)
                    if kt == QT - 1:
                        probT.used(ptk, t)
            box["o_t"] = t
            if j == XPAIRS - 1:
                xv_users[:] = [t]

        def end():
            rc, ru, rk = xr.take()
            tr = dve(lambda e: e.reciprocal(rc[:, :, :], box["sums"][:, :, 0:2]), [box["exp"]] + ru)
            row_sums.used(box["sk"], tr)
            return [lambda: copy(), lambda: finish(tr, rc, rk)]

        def copy():
            o, ou, ok = OTs.take()
            box["copied"] = act(lambda e: e.activation(o[:, :], box["O"][:, :], ACT.Copy), [box["o_t"]] + ou)
            attn.used(box["ok"], box["copied"])
            box["copy"] = o, ok

        def finish(tr, rc, rk):
            o, ok = box["copy"]
            t = box["copied"]
            J, users, jk = proj.take()
            for a in range(TILES):
                t2 = pe(lambda e, a=a: e.transpose(J[:, a * P:(a + 1) * P], o[:, a * P:(a + 1) * P], ident[:, :]),
                        [t] + users, a == TILES - 1)
            OTs.used(ok, t2)
            y, yu, yk = tmp.take()
            heads4 = lambda a: a.rearrange("p (a r d) -> p a r d", a=TILES, r=2)
            t3 = dve(lambda e: e.tensor_tensor(
                heads4(y[:, :]), heads4(J[:, :]),
                rc[:, :, :].rearrange("p a (r o) -> p a r o", o=1).to_broadcast([P, TILES, 2, XD]), ALU.mult),
                [t2, tr] + yu)
            proj.used(jk, t3)
            xr.used(rk, t3)
            xs = xg[:, :, j * P:(j + 1) * P]
            t4 = pool(lambda e: e.tensor_tensor(xs, xs, y[:, :].rearrange("p (a n) -> p a n", a=TILES), ALU.add),
                      [t3, xg_loaded[j]])
            tmp.used(yk, t4)
            stored = q.dma(x2_lanes[j], cols(x2, g, j), xs, [t4])
            x2_stored.append(stored)
            if g + 1 < NG:
                xg_loaded[j] = q.dma(xg_lanes[j], xs, cols(x1, g + 1, j), [stored])
        return dict(heads=n_heads, scale=XD ** -0.5, set=2, box=box, begin=begin, scores=mk_scores, sums=sums,
                    values=values, end=end)

    def low_rank(state, w, waits):
        J, users, jk = proj.take()
        t = down_three(J, users, w, state["parts"], state["ready"] + waits)
        actT.used(state["k"], t)
        return lambda hi, lo, hl_users: split_bank(J, jk, t, hi, lo, hl_users)

    def v_up(kv, kv_ok, m, n):
        J, users, jk = proj.take()
        for part in range(2):
            t = pe(lambda e, part=part: e.matmul(
                J[:, :], kv[:, part, m * P:(m + 1) * P], wvu[:, n * GT:(n + 1) * GT],
                start=part == 0, stop=part == 1), kv_ok + [wvu_ok] + users, part == 1)
        dst = xv[:, m, n * GT:(n + 1) * GT]
        if n:
            t = act(lambda e: e.activation(dst, J[:, :], ACT.Copy), [t] + xv_users)
        else:
            t = dve(lambda e: e.tensor_copy(dst, J[:, :]), [t] + xv_users)
        proj.used(jk, t)
        return t

    def xq_piece(j, stacks, cq_ok):
        def mm():
            J, users, jk = proj.take()
            for n, (wp, ap) in enumerate(((0, 0), (0, 1), (1, 0))):
                t = pe(lambda e, wp=wp, ap=ap, n=n: e.matmul(
                    J[:, :], wqk[wp][:, j * P:(j + 1) * P], cq[:, ap, :], start=n == 0, stop=n == 2),
                    cq_ok + wqk_ok + users, n == 2)
            if j == XPAIRS - 1:
                cq_users[:] = [t]

            def rest():
                b, bu, bk = hl.take()
                th, tl = split_bank(J, jk, t, b[:, 0, :], b[:, 1, :], bu)
                st, su, sk = xst.take()
                for part, tok in ((0, th), (1, tl)):
                    for r in range(2):
                        t2 = q.dma(xst_lanes[sk], st[part * XD:(part + 1) * XD, r, :].bitcast(F32),
                                   b[r * XD:(r + 1) * XD, part, :].bitcast(F32), [tok] + su)
                hl.used(bk, t2)
                stacks[j] = (st, sk, t2)
            return rest
        return mm

    def group_inputs(g):
        xs, x_preps, x_turns = turned_group(g, x1, list(x1_stored.values()), True)
        cs, c_preps, c_turns = turned_group(g, ctx_in, [], False)
        return xs, cs, x_preps + c_preps, x_turns + c_turns

    xs, cs, preps, turns = group_inputs(0)
    preps[0]()
    preps[1]()
    for i in range(2 * TILES):
        run(turns[2 * i])
        run(turns[2 * i + 1])
        if i + 2 < 2 * TILES:
            preps[i + 2]()
    late = []
    for g in range(NG):
        cq_split = low_rank(xs, lambda wp, kb: wqd[wp][:, kb, :], wqd_ok)
        ckv_split = low_rank(cs, lambda wp, kb: wkv[wp][:, kb, :, :].rearrange("p c n -> p (c n)"), wkv_ok)
        cq_ok = cq_split(cq[:, 0, :], cq[:, 1, :], cq_users)
        kv, ku, kvk = ckv.take()
        kv_ok = ckv_split(kv[:, 0, :], kv[:, 1, :], ku)
        for f in late:
            f()
        if g + 1 < NG:
            xs, cs, preps, turns = group_inputs(g + 1)
            preps[0]()
            preps[1]()
        stacks = {}
        for j in range(2):
            run(xq_piece(j, stacks, cq_ok))
        v_ok = [v_up(kv, kv_ok, m, n) for m in range(TILES) for n in range(2)]

        plan = {}
        for j in range(XPAIRS):
            if j + 2 < XPAIRS:
                plan[j, 1] = [xq_piece(j + 2, stacks, cq_ok)]
            if g + 1 < NG:
                plan[j, 0] = [turns[2 * j]]
                plan[j, 3] = [turns[2 * j + 1]] + ([preps[j + 2]] if j + 2 < len(preps) else [])
        units = [{"heads": 2 * GB, "make": lambda j=j: cross_unit(g, j, kv, kvk, kv_ok, v_ok, stacks)}
                 for j in range(XPAIRS)]
        late = attention(units, lambda n: plan.get(divmod(n, 2 * GB), []))
    for f in late:
        f()
    q.phase_end()
    mem.close()

    mem = ExitStack()
    half_tok = TOK // 2
    HB = half_tok // GT
    parts3 = [sb(f"hT3_{n}", [P, KB, GT], F32R, mem) for n in ("hi", "lo")]
    actT = Ring([parts3])
    u1s = [sb(f"u1_{n}", [P, KB, RANK], F32R, mem) for n in ("hi", "lo")]
    v2s = [sb(f"v2_{n}", [P, RB, D], F32R, mem) for n in ("hi", "lo")]
    pT = [sb(f"pT_{n}", [P, RB, TOK], F32R, mem) for n in ("hi", "lo")]
    wraw = Ring([sb(f"w_raw{i}", [P, 3 * RANK], F32, mem) for i in range(3)])
    wsplit = Ring([(sb(f"w_hi{i}", [P, 3 * RANK], F32R, mem), sb(f"w_lo{i}", [P, 3 * RANK], F32R, mem))
                   for i in range(2)])
    gated = Ring([sb(f"gated{i}", [P, GT], F32, mem) for i in range(2)])
    inner = Ring([sb(f"inner{i}", [P, GT], F32, mem) for i in range(2)])
    inner_hl = Ring([sb(f"inner_hl{i}", [P, 2, GT], F32R, mem) for i in range(2)])
    zT = [sb(f"zT_{n}", [P, RB, half_tok], F32R, mem) for n in ("hi", "lo")]
    b1_rows = sb("b1_rows", [2 * FB, P], F32, mem)
    b1c = sb("b1_cols", [P, 2 * FB], F32, mem)
    b2_all = sb("b2_all", [P, D], F32, mem)
    b1_lane, b2_lane = q.lane("b1_loaded"), q.lane("b2_loaded")
    wraw_lanes = [q.lane(f"w_raw{i}_loaded") for i in range(3)]
    out_lanes = [q.lane(f"out_stored{i}") for i in range(3)]

    t = pool(lambda e: e.memset(b1_rows[:, :], 0.0))
    for i in range(2):
        t2 = q.dma(b1_lane, b1_rows[i * FB:i * FB + FB - 1, :],
                   b1[i * INTER:i * INTER + (FB - 1) * P].rearrange("(a b) -> a b", b=P), [t])
        t2 = q.dma(b1_lane, b1_rows[i * FB + FB - 1:i * FB + FB, 0:FLAST],
                   b1[i * INTER + (FB - 1) * P:(i + 1) * INTER].rearrange("(a b) -> a b", a=1), [t])
    J, users, jk = proj.take()
    t = pe(lambda e, J=J: e.transpose(J[:, 0:2 * FB], b1_rows[:, :], ident[0:2 * FB, 0:2 * FB]), [t2] + users, True)
    b1_ok = dve(lambda e, J=J: e.tensor_copy(b1c[:, :], J[:, 0:2 * FB]), [t])
    proj.used(jk, b1_ok)
    b2_ok = q.dma(b2_lane, b2_all[:, :], b2.rearrange("(o n) -> o n", o=1).to_broadcast([P, D]))

    u1_ok, v2_ok = [], []
    for i in range(2):
        buf, k, t = load_into(u1[i * 4 * P:(i + 1) * 4 * P, :].rearrange("(k p) n -> p k n", p=P),
                              lambda b: b[:, :].rearrange("p (k n) -> p k n", k=4))
        ok = split_weight(u1s[0][:, 4 * i:4 * i + 4, :], u1s[1][:, 4 * i:4 * i + 4, :],
                          buf[:, :].rearrange("p (k n) -> p k n", k=4), [t])
        xin.used(k, *ok)
        u1_ok += ok
    for i in range(RB):
        buf, k, t = load_into(rows(v2, i), lambda b: b[:, :])
        ok = split_weight(v2s[0][:, i, :], v2s[1][:, i, :], buf[:, :], [t])
        xin.used(k, *ok)
        v2_ok += ok

    p_ok = {}

    def rank_down(g):
        state, preps, turns = turned_group(g, x2, x2_stored, True)
        for m in range(TILES):
            preps[m]()
            run(turns[2 * m])
            run(turns[2 * m + 1])
        parts, ak, ready = state["parts"], state["k"], state["ready"]
        p_ok[g] = []
        for r in range(RB):
            J, users, jk = proj.take()
            t = down_three(J, users, lambda wp, kb: u1s[wp][:, kb, r * P:(r + 1) * P], parts, ready + u1_ok)
            p_ok[g] += split_bank(J, jk, t, pT[0][:, r, g * GT:(g + 1) * GT], pT[1][:, r, g * GT:(g + 1) * GT], [])
        actT.used(ak, t)

    gate_up = Ring([bank[0], bank[1]] + [bank[2], bank[3]])
    z_banks = [bank[4], bank[5], bank[6], bank[7]]
    def bank_users(ring, k):
        return list(ring.users[k])

    z_users = [[], [], [], []]
    z_ready = []
    zT_users = []

    def inner_weights(f):
        raw, users, k = wraw.take()
        n = P if f < FB - 1 else FLAST
        w = list(users)
        if n < P:
            w.append(pool(lambda e: e.memset(raw[:, :], 0.0), users))
        g4 = raw[:, 0:2 * RANK].rearrange("p (s r n) -> p s r n", s=2, r=RB)
        for s in range(2):
            c = s * INTER + f * P
            t = q.dma(wraw_lanes[k], g4[:, s, :, 0:n], v1[:, c:c + n].rearrange("(r p) n -> p r n", p=P), w)
        t = q.dma(wraw_lanes[k], raw[0:n, 2 * RANK:3 * RANK], u2[f * P:f * P + n, :], w)
        (hi, lo), su, sk = wsplit.take()
        th = pool(lambda e: e.tensor_scalar(hi[:, :], raw[:, :], 1.0, 0.0, ALU.mult, ALU.add), [t] + su)
        tl = pool(lambda e: e.tensor_tensor(lo[:, :], raw[:, :], hi[:, :].bitcast(F32), ALU.subtract), [th] + su)
        wraw.used(k, tl)
        return (hi, lo), sk, [th, tl]

    PASSES = ((0, 0), (0, 1), (1, 0))

    def gate_up_stage(f, g, w, w_ok):
        banks = []
        for s in range(2):
            G, gu, gk = gate_up.take()
            for r in range(RB):
                for n, (wp, ap) in enumerate(PASSES):
                    c = (s * RB + r) * P
                    last = r == RB - 1 and n == 2
                    t = pe(lambda e, G=G, r=r, n=n, wp=wp, ap=ap, c=c, last=last: e.matmul(
                        G[:, :], w[wp][:, c:c + P], pT[ap][:, r, g * GT:(g + 1) * GT],
                        start=r == 0 and n == 0, stop=last), w_ok + p_ok[g] + gu, last)
            banks.append((G, gk, t))
        (G, gk, tg), (U, uk, tu) = banks
        sg, sgu, sgk = gated.take()
        t = act(lambda e: e.activation(sg[:, :], G[:, :], ACT.Silu, bias=b1c[:, f:f + 1]), [tg, b1_ok] + sgu)
        gate_up.used(gk, t)
        a, au, ak = inner.take()
        t = dve(lambda e: e.scalar_tensor_tensor(a[:, :], U[:, :], b1c[:, FB + f:FB + f + 1], sg[:, :],
                                                 ALU.add, ALU.mult), [t, tu] + au)
        gate_up.used(uk, t)
        gated.used(sgk, t)
        b, bu, bk = inner_hl.take()
        th = act(lambda e: e.activation(b[:, 0, :], a[:, :], ACT.Copy), [t] + bu)
        tl = dve(lambda e: e.tensor_tensor(b[:, 1, :], a[:, :], b[:, 0, :].bitcast(F32), ALU.subtract), [th] + bu)
        inner.used(ak, tl)
        return b, bk, [th, tl]

    def z_stage(f, gi, b, bk, b_ok, w, wk_, w_ok, last_use):
        for r in range(RB):
            Z = z_banks[gi * RB + r]
            for n, (wp, ap) in enumerate(PASSES):
                c = 2 * RANK + r * P
                t = pe(lambda e, Z=Z, n=n, wp=wp, ap=ap, c=c: e.matmul(
                    Z[:, :], w[wp][:, c:c + P], b[:, ap, :], start=f == 0 and n == 0, stop=f == FB - 1 and n == 2,
                    skip_group_check=True), b_ok + w_ok + z_users[gi * RB + r], r == RB - 1 and n == 2)
        inner_hl.used(bk, t)
        if last_use:
            wsplit.used(wk_, t)
        return t

    for half in range(2):
        for gi in range(HB):
            rank_down(half * HB + gi)
        everyone = [u for ring in (scores, turned, attn, proj) for us in ring.users for u in us]
        if half == 0:
            for k in range(4):
                gate_up.users[k] += everyone
        for k in range(4):
            z_users[k] = list(everyone)
        steps = [(f, gi) for f in range(FB) for gi in range(HB)]
        loaded = {0: inner_weights(0)}
        pending = []
        for f, gi in steps:
            w, wsk, w_ok = loaded[f]
            b, bk, b_ok = gate_up_stage(f, half * HB + gi, w, w_ok)
            pending.append((f, gi, b, bk, b_ok, w, wsk, w_ok, gi == HB - 1))
            if len(pending) > 1:
                t = z_stage(*pending.pop(0))
            if gi == 0 and f + 1 < FB:
                loaded[f + 1] = inner_weights(f + 1)
        t = z_stage(*pending.pop(0))
        z_ok = []
        for gi in range(HB):
            for r in range(RB):
                Z = z_banks[gi * RB + r]
                hi, lo = (zT[n][:, r, gi * GT:(gi + 1) * GT] for n in range(2))
                th = act(lambda e, Z=Z, hi=hi: e.activation(hi, Z[:, :], ACT.Copy), [t] + zT_users)
                tl = dve(lambda e, Z=Z, hi=hi, lo=lo: e.tensor_tensor(lo, Z[:, :], hi.bitcast(F32), ALU.subtract),
                         [th] + zT_users)
                z_ok += [th, tl]
        for ring in (turned, attn, proj):
            for k in range(len(ring.bufs)):
                ring.used(k, *z_ok)
        for m in range(half_tok // P):
            tile = half * (half_tok // P) + m
            buf, k, loaded_t = load_rows(rows(x2, tile), x2_stored)
            tb = pool(lambda e, buf=buf: e.tensor_tensor(buf[:, :], buf[:, :], b2_all[:, :], ALU.add),
                      [loaded_t, b2_ok])
            for n in range(2):
                J, users, jk = proj.take()
                for r in range(RB):
                    for i, (wp, ap) in enumerate(PASSES):
                        last = r == RB - 1 and i == 2
                        t = pe(lambda e, J=J, r=r, i=i, wp=wp, ap=ap, n=n, m=m, last=last: e.matmul(
                            J[:, :], zT[ap][:, r, m * P:(m + 1) * P], v2s[wp][:, r, n * GT:(n + 1) * GT],
                            start=r == 0 and i == 0, stop=last), z_ok + v2_ok + users, last)
                xs = buf[:, n * GT:(n + 1) * GT]
                t2 = dve(lambda e, J=J, xs=xs: e.tensor_tensor(xs, J[:, :], xs, ALU.add), [t, tb])
                proj.used(jk, t2)
            zT_users = [t]
            t3 = q.dma(out_lanes[k], rows(out, tile), buf[:, :], [t2])
            xin.used(k, t3)
    q.phase_end()
    ends = list(q.gate["sync"])
    mem.close()

    with nc.Block() as block:
        @block.sync
        def _(eng):
            q.emit("sync", eng)
            for sem, value in ends:
                eng.wait_ge(sem, value)

        @block.tensor
        def _(eng):
            q.emit("tensor", eng)

        @block.scalar
        def _(eng):
            q.emit("scalar", eng)

        @block.vector
        def _(eng):
            q.emit("vector", eng)

        @block.gpsimd
        def _(eng):
            q.emit("gpsimd", eng)
    ctx.close()


_INS = ["x", "ctx_4096", "L0_attn_q_weight", "L0_attn_q_scale", "L0_attn_k_weight", "L0_attn_k_scale",
        "L0_attn_v_weight", "L0_attn_v_scale", "L0_attn_o_weight", "L0_attn_o_scale", "L0_xattn_Wq_d",
        "L0_xattn_W_qk", "L0_xattn_Wkv_d", "L0_xattn_Wv_u", "L0_ffn_U1", "L0_ffn_V1", "L0_ffn_U2", "L0_ffn_V2",
        "L0_ffn_b1", "L0_ffn_b2"]


def kernel(**inputs):
    import concourse.bacc as bacc
    import numpy as np
    from concourse.bass_utils import run_bass_kernel_spmd

    nc = bacc.Bacc("TRN2", target_bir_lowering=False, num_devices=1)
    arrays, args = {}, []
    for name in _INS:
        a = np.ascontiguousarray(inputs[name])
        if name in ("x", "ctx_4096"):
            a = a.reshape(TOK, D)
        arrays[f"in_{name}"] = a
        args.append(nc.dram_tensor(f"in_{name}", a.shape, mybir.dt.from_np(a.dtype), kind="ExternalInput").ap())
    args.append(nc.dram_tensor("out", (TOK, D), F32, kind="ExternalOutput").ap())
    build_program(nc, *args)
    r = run_bass_kernel_spmd(nc, [arrays], core_ids=[0])
    return r.results[0]["out"].reshape(BATCH, SEQ, D)
```

```python
from contextlib import ExitStack

import concourse.bass as bass
from concourse import mybir

F32 = mybir.dt.float32
F32R = mybir.dt.float32r
F16 = mybir.dt.float16
ALU = mybir.AluOpType
ACT = mybir.ActivationFunctionType
AX = mybir.AxisListType

BATCH, SEQ, D = 8, 256, 1024
P = 128
TOK = BATCH * SEQ
KB = D // P
GT = 512
NG = TOK // GT
TILES = GT // P
GB = GT // SEQ
QT = SEQ // P
HEADS, KV_HEADS = 32, 8
HD = D // HEADS
REP = HEADS // KV_HEADS
KVD = KV_HEADS * HD
XH, XD = 16, 64
XPAIRS = XH // 2
LQ = 128
INTER, RANK = 2752, 256
RB = RANK // P
FB = (INTER + P - 1) // P
FLAST = INTER - (FB - 1) * P
LN_EPS = 1e-5
SIGN_EPS = 1e-8
PASSES = ((0, 0), (0, 1), (1, 0))
ON_SCALAR_SELF, ON_SCALAR_CROSS = (1, 4, 6), (1, 3, 5, 7)


class Queues:

    ENGINES = ("tensor", "scalar", "vector", "gpsimd", "sync")

    def __init__(self, nc, ctx):
        self.nc, self.ctx = nc, ctx
        self.queue = {e: [] for e in self.ENGINES}
        self.done = {e: ctx.enter_context(nc.semaphore(f"{e}_done")) for e in self.ENGINES[:4]}
        self.count = {e: 0 for e in self.ENGINES}
        self.gate = {e: [] for e in self.ENGINES}
        self.lanes = []

    def op(self, engine, build, waits=(), signal=True):
        waits = self.gate[engine] + list(waits)
        self.gate[engine] = []
        token = None
        if signal:
            self.count[engine] += 1
            token = (self.done[engine], self.count[engine])
        self.queue[engine].append((waits, build, token and token[0], 1))
        return token

    def lane(self, name):
        lane = [self.ctx.enter_context(self.nc.semaphore(name)), 0]
        self.lanes.append(lane)
        return lane

    def dma(self, lane, out, in_, waits=()):
        waits = self.gate["sync"] + list(waits)
        self.gate["sync"] = []
        lane[1] += 16
        self.queue["sync"].append((waits, lambda e: e.dma_start(out, in_), lane[0], 16))
        return (lane[0], lane[1])

    def phase_end(self, apart=()):
        last = [(self.done[e], self.count[e]) for e in self.ENGINES[:4] if self.count[e]]
        last += [(lane[0], lane[1]) for lane in self.lanes if lane[1] and lane not in apart]
        for e in self.ENGINES[1:]:
            self.gate[e] = list(last)

    def emit(self, engine, eng):
        passed = {}
        for waits, build, sem, by in self.queue[engine]:
            for token in waits:
                if token is not None and passed.get(id(token[0]), 0) < token[1]:
                    eng.wait_ge(token[0], token[1])
                    passed[id(token[0])] = token[1]
            ins = build(eng)
            if sem is not None:
                ins.then_inc(sem, by)


class Ring:

    def __init__(self, bufs):
        self.bufs, self.users, self.free = bufs, [[] for _ in bufs], list(range(len(bufs)))

    def take(self):
        k = self.free.pop(0)
        users, self.users[k] = self.users[k], []
        return self.bufs[k], users, k

    def used(self, k, *tokens):
        if k not in self.free:
            self.free.append(k)
        self.users[k] += tokens


def build_program(nc, x, ctx_in, wq, qs, wk, ks, wv, vs, wo, os_, wq_d, w_qk, wkv_d, wv_u,
                  u1, v1, u2, v2, b1, b2, out):
    ctx = ExitStack()
    q = Queues(nc, ctx)
    pe = lambda f, waits=(), signal=False: q.op("tensor", f, waits, signal)
    act = lambda f, waits=(), signal=True: q.op("scalar", f, waits, signal)
    dve = lambda f, waits=(), signal=True: q.op("vector", f, waits, signal)
    pool = lambda f, waits=(), signal=True: q.op("gpsimd", f, waits, signal)

    def sb(name, shape, dt, where=ctx):
        return where.enter_context(nc.sbuf_tensor(name, shape, dt))

    x1 = nc.dram_tensor("x1_scratch", [TOK, D], F32, kind="Internal").ap()
    x2 = nc.dram_tensor("x2_scratch", [TOK, D], F32, kind="Internal").ap()
    rows = lambda a, tile: a[tile * P:(tile + 1) * P, :]

    ident = sb("ident", [P, P], F32)
    neg_half = sb("neg_half", [P, 1], F32)
    xin = Ring([sb(f"xin{i}", [P, D], F32) for i in range(3)])
    xin_lane = [q.lane(f"xin{i}_loaded") for i in range(3)]
    xres = Ring([sb(f"x_res{i}", [P, D], F32) for i in range(2)])
    xres_lanes = [q.lane(f"x_res{i}_loaded") for i in range(2)]
    store_lanes = [q.lane(f"x_res{i}_stored") for i in range(2)]
    bn = Ring([sb(f"bn{i}", [P, 16], F32) for i in range(2)])
    attn_mem = ExitStack()
    ident16 = sb("ident16", [P, P], F16, attn_mem)
    ones = sb("ones", [P, P], F32, attn_mem)
    prob = Ring([sb(f"prob{i}", [P, GT], F32, attn_mem) for i in range(3)])
    probT = Ring([sb(f"probT{i}", [P, GT], F32, attn_mem) for i in range(6)])
    tmp = Ring([sb(f"tmp{i}", [P, GT], F32, attn_mem) for i in range(2)])
    maxes = Ring([sb(f"neg_max{i}", [P, QT], F32, attn_mem) for i in range(4)])
    row_sums = Ring([sb(f"row_sums{i}", [P, 4, REP], F32, attn_mem) for i in range(3)])

    bank = [ctx.enter_context(nc.psum_tensor(f"bank{i}", [P, GT], F32)) for i in range(8)]
    scores = Ring(bank[0:3])
    turned = Ring(bank[3:5])
    attn = Ring(bank[5:6])
    proj = Ring(bank[6:8])

    c0 = pool(lambda e: e.memset(ident[:, :], 0.0))
    c1 = pool(lambda e: e.affine_select(out=ident[:, :], in_=ident[:, :], compare_op=ALU.not_equal, fill=1.0,
                                        base=0, pattern=[[-1, P]], channel_multiplier=1), [c0])
    ident_ok = pool(lambda e: e.tensor_copy(ident16[:, :], ident[:, :]), [c1])
    ones_ok = pool(lambda e: e.memset(ones[:, :], 1.0))
    half_ok = pool(lambda e: e.memset(neg_half[:, :], -0.5))

    tiles_in, residuals = (xin, xin_lane), (xres, xres_lanes)

    def load_rows(src, waits=(), into=tiles_in):
        ring, lanes = into
        buf, users, k = ring.take()
        token = q.dma(lanes[k], buf[:, :], src, list(users) + list(waits))
        return buf, (lambda *readers: ring.used(k, *readers)), token

    def layernorm(buf, loaded):
        st, users, sk = bn.take()
        t = [dve(lambda e, i=i: e.bn_stats(st[:, 6 * i:6 * i + 6], buf[:, GT * i:GT * (i + 1)]),
                 [loaded] + users) for i in range(2)]
        t = dve(lambda e: e.bn_aggr(st[:, 12:14], st[:, 0:12]), t)
        dve(lambda e: e.tensor_scalar(st[:, 12:13], st[:, 12:13], -1.0, None, ALU.mult), [t], False)
        t = dve(lambda e: e.tensor_scalar(st[:, 14:15], st[:, 13:14], LN_EPS, None, ALU.add), [t])
        t = pool(lambda e: e.tensor_tensor(st[:, 15:16], st[:, 14:15], neg_half[:, :], ALU.pow), [t, half_ok])
        t = pool(lambda e: e.tensor_scalar(buf[:, :], buf[:, :], st[:, 12:13], st[:, 15:16], ALU.add, ALU.mult), [t])
        bn.used(sk, t)
        return t

    def transpose_tile(src, ready, hi, lo, m, waits, used):
        pieces = []
        for half in range(2):
            def mm(half=half):
                J, users, jk = proj.take()
                for i in range(4):
                    kb = 4 * half + i
                    t = pe(lambda e, i=i, kb=kb: e.transpose(J[:, i * P:(i + 1) * P], src[:, kb * P:(kb + 1) * P],
                                                             ident[:, :]),
                           [ready, ident_ok] + users, signal=i == 3)
                used(t)

                def split():
                    J3 = J[:, :].rearrange("p (k n) -> p k n", k=4)
                    dst = lambda a: a[:, 4 * half:4 * half + 4, m * P:(m + 1) * P]
                    th = act(lambda e: e.activation(dst(hi), J3, ACT.Copy), [t] + waits)
                    tl = dve(lambda e: e.tensor_tensor(dst(lo), J3, as_f32(dst(hi)), ALU.subtract), [th] + waits)
                    proj.used(jk, tl)
                    return [th, tl]
                return split
            pieces.append(mm)
        return pieces

    def as_f32(a):
        return a.bitcast(F32) if a.dtype == F32R else a

    def run(piece):
        rest = piece()
        return rest() if rest else None

    def score_stage(mms):
        S, users, sk = scores.take()
        t = mms(S, users)
        mx, mu, mk = maxes.take()
        S3 = S[:, :].rearrange("p (a b) -> p a b", a=QT)
        t = dve(lambda e: e.tensor_reduce(mx[:, 0:QT], S3, AX.X, ALU.max, negate=True), [t] + mu)
        return S, sk, mx, mk, t

    def exp_stage(S, sk, mx, mk, t, sums):
        Pb, pu, pk = prob.take()
        te = [act(lambda e, a=a, total=sums(a): e.activation(
                      Pb[:, a * SEQ:(a + 1) * SEQ], S[:, a * SEQ:(a + 1) * SEQ], ACT.Exp,
                      bias=mx[:, a:a + 1], accum_out=total),
                  [t] + pu) for a in range(QT)]
        scores.used(sk, te[-1])
        maxes.used(mk, te[-1])
        return Pb, pk, te

    def turn_stage(Pb, pk, te):
        T, users, tk = turned.take()
        for kt in range(QT):
            for qt in range(QT):
                t = pe(lambda e, kt=kt, qt=qt: e.transpose(
                    T[:, kt * SEQ + qt * P:kt * SEQ + (qt + 1) * P],
                    Pb[:, qt * SEQ + kt * P:qt * SEQ + (kt + 1) * P], ident[:, :]),
                    te + users, signal=kt == QT - 1 and qt == QT - 1)
        prob.used(pk, t)
        return T, tk, t

    def evac_stage(T, tk, t, n, on_scalar):
        PT, ptu, ptk = probT.take()
        if n % 8 in on_scalar:
            t = act(lambda e: e.activation(PT[:, :], T[:, :], ACT.Copy), [t] + ptu)
        else:
            t = dve(lambda e: e.tensor_copy(PT[:, :], T[:, :]), [t] + ptu)
        turned.used(tk, t)
        return PT, ptk, t

    AHEAD = 3

    def attention(units, side_work, lead):
        heads = [(u, i) for u in units for i in range(u["heads"])]
        scored, soft, ready, rest = {}, {}, {}, []

        def score(n):
            if n < len(heads):
                u, i = heads[n]
                if i == 0:
                    u.update(u.pop("make")())
                    u["begin"]()
                scored[n] = score_stage(lambda S, w: u["scores"](i, S, w))

        def exp(n):
            if n < len(heads):
                u, i = heads[n]
                soft[n] = exp_stage(*scored.pop(n), lambda a: u["sums"](i, a))
                u["box"]["exp"] = soft[n][2][-1]

        for n in range(AHEAD):
            score(n)
        exp(0)
        for piece in lead:
            run(piece)
        finish = []
        for n in range(len(heads) + 1):
            score(n + AHEAD)
            if n < len(heads):
                T = turn_stage(*soft.pop(n))
                exp(n + 1)
                ready[n] = evac_stage(*T, n, heads[n][0]["on_scalar"])
            for r in rest:
                r()
            rest = []
            for piece in side_work(n):
                r = piece()
                if r:
                    rest.append(r)
            if finish:
                finish.pop(0)()
            if n >= 1:
                u, i = heads[n - 1]
                s = u["set"]
                if i % s == s - 1:
                    u["values"](i // s, [ready.pop(n - s + j) for j in range(s)])
                if i == u["heads"] - 1:
                    finish += u["end"]()
        return rest + finish

    mem = ExitStack()
    sW = sb("signs_qkv", [P, KB, D + 2 * KVD], F16, mem)
    sWo = sb("signs_o", [P, KB, D], F32R, mem)
    NSC = (2 * D + 2 * KVD) // P
    QB, VB, OB = KB, KB + KVD // P, KB + 2 * KVD // P
    sc_rows = sb("scale_rows", [NSC, P], F32, mem)
    sc = sb("scale_cols", [P, NSC], F32, mem)
    abs_sum = sb("abs_sum", [P, NSC], F32, mem)
    s_mean = sb("s_mean", [P, NSC], F32, mem)
    chan = sb("channel_scale", [P, NSC], F32, mem)
    cv = sb("v_scale_all", [P, KVD], F32, mem)
    co = sb("o_scale_all", [P, D], F32, mem)
    sign_ring = Ring([sb(f"sign{i}", [P, D], F16, mem) for i in range(2)])
    hT_hi = sb("hT_hi", [P, KB, GT], F16, mem)
    hT_lo = sb("hT_lo", [P, KB, GT], F16, mem)
    kst = sb("k_stack", [P, KV_HEADS, GT], F32R, mem)
    vall = sb("v_all", [P, TILES, KVD], F32, mem)
    hl = Ring([sb(f"hi_lo{i}", [P, 2, GT], F32R, mem) for i in range(2)])
    qst = Ring([sb(f"q_stack{i}", [P, REP, GT], F32R, mem) for i in range(2)])
    OT_hi = sb("attnT_hi", [P, KB, GT], F32R, mem)
    OT_lo = sb("attnT_lo", [P, KB, GT], F32R, mem)
    r_all = sb("recip_all", [P, 4, REP, HD], F32, mem)
    R_sb = sb("recipT", [P, GT], F32, mem)
    OTn = sb("attnT", [P, GT], F32, mem)
    sc_lane = q.lane("scales_loaded")
    st_lanes = [q.lane(f"stack{i}_loaded") for i in range(2)]
    k_lanes = [q.lane(f"k_stack{i}_loaded") for i in range(2)]

    zeroed = []

    t = None
    for src, n, at in ((qs, KB, 0), (ks, KVD // P, QB), (vs, KVD // P, VB), (os_, KB, OB)):
        t = q.dma(sc_lane, sc_rows[at:at + n, :], src.rearrange("(a b) -> a b", b=P))
    J, users, jk = proj.take()
    t = pe(lambda e, J=J: e.transpose(J[:, 0:NSC], sc_rows[:, :], ident[0:NSC, 0:NSC]), [t, ident_ok], True)
    sc_ok = dve(lambda e, J=J: e.tensor_copy(sc[:, :], J[:, 0:NSC]), [t])
    proj.used(jk, sc_ok)

    chan_ok = {}
    signs_ok = {}

    def sign_pieces(src, tile, idx, dst, at):
        box = {}
        c = slice(idx, idx + 1)

        def load():
            box["w"], box["read"], box["loaded"] = load_rows(rows(src, tile))

        def mean():
            sg, sgu, box["sk"] = sign_ring.take()
            box["sg"] = sg
            t = act(lambda e: e.activation(sg[:, :], box["w"][:, :], ACT.Abs, accum_out=abs_sum[:, c]),
                    [box["loaded"]] + sgu)
            box["abs"] = t
            t = dve(lambda e: e.tensor_scalar(s_mean[:, c], abs_sum[:, c], 1.0 / D, SIGN_EPS, ALU.mult, ALU.max), [t])
            factor = HD ** -0.5 if idx < QB else 1.0
            chan_ok[idx] = dve(lambda e: e.scalar_tensor_tensor(chan[:, c], s_mean[:, c], factor, sc[:, c],
                                                                ALU.mult, ALU.mult), [t, sc_ok])

        def sign():
            t = act(lambda e: e.activation(box["sg"][:, :], box["w"][:, :], ACT.Sign), [box["abs"]])
            box["t"] = t
            box["read"](t)

        def mm():
            J, users, jk = proj.take()
            J16 = J[:, :].bitcast(F16)
            for kb in range(KB):
                tt = pe(lambda e, kb=kb: e.transpose(J16[:, kb * P:(kb + 1) * P], box["sg"][:, kb * P:(kb + 1) * P],
                                                     ident16[:, :]), [box["t"], ident_ok] + users, kb == KB - 1)
            sign_ring.used(box["sk"], tt)

            def evac():
                J3 = J16.rearrange("p (k n) -> p k n", k=KB)
                signs_ok[idx] = dve(lambda e: e.tensor_copy(dst[:, :, at:at + P], J3), [tt])
                proj.used(jk, signs_ok[idx])
            return evac
        return load, mean, sign, mm

    def scale_all(first, n, dst):
        last = None
        for half in range((n + 3) // 4):
            J, users, jk = proj.take()
            m = min(4, n - 4 * half)
            for i in range(m):
                idx = first + 4 * half + i
                dg, du, dk = tmp.take()
                t = dve(lambda e, idx=idx, dg=dg: e.tensor_scalar(dg[:, 0:P], ident[:, :], chan[:, idx:idx + 1], None,
                                                                  ALU.mult), [chan_ok[idx], ident_ok] + du)
                t = pe(lambda e, i=i, dg=dg, J=J: e.matmul(J[:, i * P:(i + 1) * P], ones[:, :], dg[:, 0:P],
                                                           start=True, stop=True), [t, ones_ok] + users, True)
                tmp.used(dk, t)
            last = dve(lambda e, half=half, m=m, J=J: e.tensor_copy(dst[:, half * GT:half * GT + m * P],
                                                                    J[:, 0:m * P]), [t])
            proj.used(jk, last)
        return last

    hT_users = []
    hT_ready = []
    kst_users, v_users, OT_users = [], [], []

    def ln_pieces(g, into=lambda m: tiles_in):
        loads, norms, turns, shared = [], [], [], {}
        for m in range(TILES):
            box = {}

            def load(m=m, box=box):
                box["loaded"] = load_rows(rows(x, g * TILES + m), into=into(m))

            def norm(box=box):
                buf, read, loaded = box["loaded"]
                box["tile"] = buf, read, layernorm(buf, loaded)

            def turn(half, m=m, box=box):
                if m == 0 and half == 0:
                    shared["users"] = list(hT_users)
                    hT_users.clear()
                    hT_ready.clear()
                if half == 0:
                    buf, read, ok = box["tile"]
                    box["p"] = transpose_tile(buf, ok, hT_hi, hT_lo, m, shared["users"], read)
                r = box["p"][half]()
                return lambda: hT_ready.extend(r())
            loads.append(load)
            norms.append(norm)
            turns.append([lambda turn=turn, half=half: turn(half) for half in range(2)])
        return loads, norms, turns

    def split_scaled(J, jk, t, idx):
        b, bu, bk = hl.take()
        c = chan[:, idx:idx + 1]
        th = act(lambda e: e.activation(b[:, 0, :], J[:, :], ACT.Copy, scale=c), [t, chan_ok[idx]] + bu)
        tl = dve(lambda e: e.scalar_tensor_tensor(b[:, 1, :], J[:, :], c, b[:, 0, :].bitcast(F32),
                                                  ALU.mult, ALU.subtract), [th, chan_ok[idx]] + bu)
        proj.used(jk, tl)
        return b, bk, th, tl

    kst_ready = {}

    def k_piece(kt):
        def mm():
            J, users, jk = proj.take()
            for kb in range(KB):
                for part in (hT_hi, hT_lo):
                    last = kb == KB - 1 and part is hT_lo
                    t = pe(lambda e, kb=kb, part=part, last=last: e.matmul(
                        J[:, :], sW[:, kb, D + kt * P:D + (kt + 1) * P], part[:, kb, :],
                        start=kb == 0 and part is hT_hi, stop=last), hT_ready + users + [signs_ok[QB + kt]], last)
            hT_users.append(t)

            def rest():
                b, bk, th, tl = split_scaled(J, jk, t, QB + kt)
                lane = k_lanes[kt]
                for part, tok, at in ((0, th, (0, 1)), (1, tl, (2,))):
                    for a in at:
                        for i in range(P // HD):
                            t2 = q.dma(lane, kst[a * HD:(a + 1) * HD, kt * (P // HD) + i, :].bitcast(F32),
                                       b[i * HD:(i + 1) * HD, part, :].bitcast(F32), [tok] + kst_users + zeroed)
                hl.used(bk, t2)
                kst_ready[kt] = t2
            return rest
        return mm

    v_ready = []

    def v_piece(pair):
        def mm():
            J, users, jk = proj.take()
            for i in range(2):
                m = 2 * pair + i
                for kb in range(KB):
                    for part in (hT_hi, hT_lo):
                        last = kb == KB - 1 and part is hT_lo
                        t = pe(lambda e, i=i, m=m, kb=kb, part=part, last=last: e.matmul(
                            J[:, i * KVD:(i + 1) * KVD], part[:, kb, m * P:(m + 1) * P],
                            sW[:, kb, D + KVD:D + 2 * KVD],
                            start=kb == 0 and part is hT_hi, stop=last),
                            hT_ready + users + [signs_ok[VB], signs_ok[VB + 1]], last and i == 1)
            hT_users.append(t)

            def rest():
                cvb = cv[:, :].rearrange("p (o n) -> p o n", o=1).to_broadcast([P, 2, KVD])
                t2 = dve(lambda e: e.tensor_tensor(vall[:, 2 * pair:2 * pair + 2, :],
                                                   J[:, :].rearrange("p (o n) -> p o n", o=2), cvb, ALU.mult),
                         [t, cv_ok[0]] + v_users)
                proj.used(jk, t2)
                v_ready.append(t2)
            return rest
        return mm

    q_ready = {}
    Q_CHUNKS = KB

    def q_pieces(g, tq, n_chunks=Q_CHUNKS):
        box = {}

        def chunk(c):
            if c == 0:
                box["J"] = proj.take()
            J, users, jk = box["J"]
            for kb in range(c * KB // n_chunks, (c + 1) * KB // n_chunks):
                for part in (hT_hi, hT_lo):
                    last = kb == KB - 1 and part is hT_lo
                    t = pe(lambda e, kb=kb, part=part, last=last: e.matmul(
                        J[:, :], sW[:, kb, tq * P:(tq + 1) * P], part[:, kb, :],
                        start=kb == 0 and part is hT_hi, stop=last), hT_ready + users + [signs_ok[tq]], last)
            if c < n_chunks - 1:
                return None
            hT_users.append(t)

            def rest():
                b, bk, th, tl = split_scaled(J, jk, t, tq)
                st, su, sk = qst.take()
                lane = st_lanes[sk]
                for part, tok, at in ((0, th, (0, 2)), (1, tl, (1,))):
                    for a in at:
                        for i in range(REP):
                            t2 = q.dma(lane, st[a * HD:(a + 1) * HD, i, :].bitcast(F32),
                                       b[i * HD:(i + 1) * HD, part, :].bitcast(F32), [tok] + su + zeroed)
                hl.used(bk, t2)
                q_ready[g, tq] = (st, sk, t2)
            return rest
        return [lambda c=c: chunk(c) for c in range(n_chunks)]

    OT_ready = {}

    def self_unit(g, tq):
        u = {"heads": GB * REP, "set": REP}
        box = {}

        def begin():
            box["q"] = q_ready[g, tq]
            box["sums"], box["su"], box["sk"] = row_sums.take()

        def mk_scores(i, S, waits):
            b, r = divmod(i, REP)
            st, sk, ready = box["q"]
            for a in range(QT):
                t = pe(lambda e, a=a: e.matmul(S[:, a * SEQ:(a + 1) * SEQ],
                                               st[:, r, b * SEQ + a * P:b * SEQ + (a + 1) * P],
                                               kst[:, tq, b * SEQ:(b + 1) * SEQ], start=True, stop=True),
                       waits + zeroed + [ready, kst_ready[tq // (P // HD)]] + box["su"], a == QT - 1)
            if i == GB * REP - 1:
                qst.used(sk, t)
                kst_users.append(t)
            return t

        def sums(i, a):
            b, r = divmod(i, REP)
            return box["sums"][:, b * QT + a, r:r + 1]

        def values(b, pts):
            if b == 0:
                box["O"], box["ou"], box["ok"] = attn.take()
            O = box["O"]
            for kt in range(QT):
                for r in range(REP):
                    PT, ptk, tp = pts[r]
                    t = pe(lambda e, kt=kt, r=r, PT=PT: e.matmul(
                        O[r * HD:(r + 1) * HD, b * SEQ:(b + 1) * SEQ], vall[:, b * QT + kt, tq * HD:(tq + 1) * HD],
                        PT[:, kt * SEQ:(kt + 1) * SEQ], start=kt == 0, stop=kt == QT - 1,
                        tile_position=(0, r * HD)), [tp] + v_ready + box["ou"], kt == QT - 1)
                    if kt == QT - 1:
                        probT.used(ptk, t)
            box["o_t"] = t

        def end():
            s = box["sums"]
            t = dve(lambda e: e.reciprocal(s[:, :, :], s[:, :, :]), [box["exp"]])
            t = pool(lambda e: e.tensor_scalar(
                r_all[:, :, :, :].rearrange("p a r d -> p (a r) d"),
                s[:, :, :].rearrange("p a (r o) -> p (a r) o", o=1).to_broadcast([P, 4 * REP, HD]),
                1.0, 0.0, ALU.mult, ALU.add), [t] + r_users)
            r_users.clear()
            row_sums.used(box["sk"], t)
            return [lambda: None, lambda: finish(t)]

        def finish(t):
            J, users, jk = proj.take()
            for a in range(4):
                t2 = pe(lambda e, a=a: e.transpose(J[:, a * P:(a + 1) * P],
                                                   r_all[:, a, :, :].rearrange("p r d -> p (r d)"), ident[:, :]),
                        [t] + users, a == 3)
            r_users.append(t2)
            t3 = act(lambda e: e.activation(R_sb[:, :], J[:, :], ACT.Copy), [t2] + R_users)
            proj.used(jk, t3)
            t4 = dve(lambda e: e.tensor_tensor(OTn[:, :], box["O"][:, :], R_sb[:, :], ALU.mult),
                     [t3, box["o_t"]] + OTn_users)
            R_users[:] = [t4]
            attn.used(box["ok"], t4)
            t5 = pool(lambda e: e.tensor_scalar(OT_hi[:, tq, :], OTn[:, :], 1.0, 0.0, ALU.mult, ALU.add),
                      [t4] + OT_users)
            t6 = pool(lambda e: e.tensor_tensor(OT_lo[:, tq, :], OTn[:, :], OT_hi[:, tq, :].bitcast(F32),
                                                ALU.subtract), [t5] + OT_users)
            OTn_users[:] = [t6]
            OT_ready[tq] = t6
            if tq == KV_HEADS - 1:
                v_users.clear()
                v_users.append(box["o_t"])
        u.update(begin=begin, scores=mk_scores, sums=sums, values=values, end=end, box=box)
        return u

    r_users, R_users, OTn_users = [], [], []

    def o_pieces(g):
        pieces, loads = [], []
        ready = {}
        for m in range(TILES):
            box = {}

            def load(m=m, box=box):
                box["x"], users, box["k"] = xres.take()
                box["xl"] = q.dma(xres_lanes[box["k"]], box["x"][:, :], rows(x, g * TILES + m), users)
            loads.append(load)
            for n in range(2):
                def mm(m=m, n=n, box=box):
                    if not ready:
                        ready.update(OT_ready)
                        OT_ready.clear()
                    J, users, jk = proj.take()
                    for tq in range(KB):
                        for part in (OT_hi, OT_lo):
                            last = tq == KB - 1 and part is OT_lo
                            t = pe(lambda e, tq=tq, part=part, last=last: e.matmul(
                                J[:, :], part[:, tq, m * P:(m + 1) * P], sWo[:, tq, n * GT:(n + 1) * GT],
                                start=tq == 0 and part is OT_hi, stop=last),
                                [ready[tq]] + users + [signs_ok[OB + i] for i in range(KB)], last)
                    if m == TILES - 1 and n == 1:
                        OT_users[:] = [t]

                    def rest():
                        y, yu, yk = tmp.take()
                        xs = box["x"][:, n * GT:(n + 1) * GT]
                        t2 = dve(lambda e: e.tensor_tensor(y[:, :], J[:, :], co[:, n * GT:(n + 1) * GT], ALU.mult),
                                 [t, co_ok[0]] + yu)
                        proj.used(jk, t2)
                        t3 = dve(lambda e: e.tensor_tensor(xs, xs, y[:, :], ALU.add), [t2, box["xl"]])
                        tmp.used(yk, t3)
                        if n == 1:
                            t4 = q.dma(store_lanes[box["k"]], rows(x1, g * TILES + m), box["x"][:, :], [t3])
                            xres.used(box["k"], t4)
                            x1_stored[g * TILES + m] = t4
                    return rest
                pieces.append(mm)
        return loads, pieces

    x1_stored = {}
    cv_ok, co_ok = [None], [None]

    signs_q = [sign_pieces(wq, i, i, sW, i * P) for i in range(KB)]
    signs_o = [sign_pieces(wo, i, OB + i, sWo, i * P) for i in range(KB)]
    first_signs = [sign_pieces(wk, i, QB + i, sW, D + i * P) for i in range(KVD // P)]
    first_signs += [signs_q[0]]
    first_signs += [sign_pieces(wv, i, VB + i, sW, D + KVD + i * P) for i in range(KVD // P)]
    first_signs += signs_q[1:3]
    loads, norms, turns = ln_pieces(0, lambda m: tiles_in if m == 2 else residuals)
    sign_items = [(sign[0], tiles_in, sign[1:3], sign[3:]) for sign in first_signs]
    tile_items = [(loads[m], tiles_in if m == 2 else residuals, norms[:2] if m == 0 else norms[m + 1:m + 2], turns[m])
                  for m in range(TILES)]
    items = [i for pair in zip(sign_items, tile_items) for i in pair] + sign_items[TILES:]
    to_load = [(i[0], i[1][0]) for i in items] + [(signs_q[3][0], xin), (signs_o[0][0], xin)]
    for k in range(len(items) + 1):
        for part in range(2):
            while to_load and to_load[0][1].free:
                to_load.pop(0)[0]()
            if part == 0 and k < len(items):
                for piece in items[k][2]:
                    piece()
            if part == 1 and k:
                for piece in items[k - 1][3]:
                    run(piece)
    while to_load:
        to_load.pop(0)[0]()
    zeroed += [pool(lambda e, a=a: e.memset(a[:, :, :].bitcast(F32), 0.0)) for a in [kst] + qst.bufs]

    def kvq_pieces(g):
        def whole(pieces):
            def mm():
                rest = None
                for p in pieces:
                    rest = p() or rest
                return rest
            return mm
        return {"k": [k_piece(kt) for kt in range(KVD // P)], "v": [v_piece(i) for i in range(TILES // 2)],
                "q": [whole(q_pieces(g, tq)) for tq in range(2)]}

    new = kvq_pieces(0)
    run(new["k"][0])
    run(new["q"][0])
    cv_ok[0] = scale_all(VB, KVD // P, cv)
    for piece in (new["v"][0], new["v"][1], new["q"][1], new["k"][1]):
        run(piece)
    cross_first = []
    o_loads, o_left = [], []
    for g in range(NG):
        units = [{"heads": GB * REP, "on_scalar": ON_SCALAR_SELF, "make": lambda tq=tq, g=g: self_unit(g, tq)}
                 for tq in range(KV_HEADS)]
        queries = {}
        plan = {}
        if o_left:
            plan[0, 1] = [o_left[1]]
        for u in range(KV_HEADS - 2):
            for i in range(Q_CHUNKS):
                def chunk(u=u, i=i, g=g, queries=queries):
                    if i == 0:
                        queries[u] = q_pieces(g, u + 2)
                    return queries[u][i]()
                at = max(0, u * GB * REP + 6 - Q_CHUNKS + i)
                plan.setdefault(divmod(at, GB * REP), []).append(chunk)
        if g == 0:
            for u in range(KV_HEADS):
                at_o = (3, 4, 7) if u + 1 < KV_HEADS else (1, 2, 4)
                for piece, i in zip(signs_o[u][1:], at_o):
                    plan.setdefault((u, i), []).append(piece)
                if u + 1 < KV_HEADS:
                    plan.setdefault((u, 5), []).append(signs_o[u + 1][0])
                if u + 3 < KB:
                    for piece, i in zip(signs_q[u + 3][1:], (0, 1, 4)):
                        plan.setdefault((u, i), []).append(piece)
                if u + 4 < KB:
                    plan.setdefault((u, 4), []).append(signs_q[u + 4][0])
        o_loads, o_work = o_pieces(g)
        last = KV_HEADS - 1
        plan.setdefault((last, 5), []).append(o_loads[0])
        plan.setdefault((last, 7), []).append(o_loads[1])
        if g + 1 < NG:
            loads, norms, turns = ln_pieces(g + 1)
            for i, piece in ((1, loads[0]), (2, loads[1]), (3, loads[2]), (4, norms[0]), (6, norms[1])):
                plan.setdefault((last, i), []).append(piece)
        lead, o_left = o_left[0:1], []
        late = attention(units, lambda n: plan.get(divmod(n, GB * REP), []), lead)
        if g == 0:
            co_ok[0] = scale_all(OB, KB, co)
        if g + 1 < NG:
            v_ready.clear()
            new = kvq_pieces(g + 1)
            order = [norms[2], *turns[0], *late, loads[3], *turns[1], o_work[0], *turns[2], norms[3], o_work[1],
                     o_loads[2], *turns[3], o_work[2], new["k"][0], new["q"][0], o_work[3], o_loads[3],
                     new["v"][0], new["v"][1], o_work[4], new["k"][1], kst_users.clear, new["q"][1], o_work[5]]
            o_left = o_work[6:]
            for piece in order:
                run(piece)
        else:
            for f in late:
                f()
            for i, piece in enumerate(o_work):
                run(piece)
                if i in (1, 3):
                    o_loads[i // 2 + 2]()
                if i < 3:
                    cross_first.append(load_rows(rows(x1, i), [x1_stored[i]]))
                if 3 <= i < 6:
                    buf, read, loaded = cross_first[i - 3]
                    cross_first[i - 3] = buf, read, layernorm(buf, loaded)
    q.phase_end(apart=store_lanes)
    mem.close()

    mem = ExitStack()
    actT = Ring([(sb(f"actT_hi{i}", [P, KB, GT], F32R, mem), sb(f"actT_lo{i}", [P, KB, GT], F32R, mem))
                 for i in range(2)])
    wqd = [sb(f"wq_down_{n}", [P, KB, LQ], F32R, mem) for n in ("hi", "lo")]
    wqk = [sb(f"w_qk_{n}", [P, XH * XD], F32R, mem) for n in ("hi", "lo")]
    wkv = [sb(f"wkv_down_{n}", [P, KB, 2, XD], F32R, mem) for n in ("hi", "lo")]
    wvu = sb("wv_up", [P, XH * XD], F32R, mem)
    cq = sb("cq_hi_lo", [P, 2, GT], F32R, mem)
    ckv = Ring([sb(f"ckv{i}", [P, 2, GT], F32R, mem) for i in range(2)])
    xv = sb("xv_all", [P, TILES, XH * XD], F32, mem)
    hl = Ring([sb(f"xhi_lo{i}", [P, 2, GT], F32R, mem) for i in range(2)])
    xst = Ring([sb(f"xq_stack{i}", [P, 2, GT], F32R, mem) for i in range(3)])
    xg = sb("x_group", [P, TILES, D], F32, mem)
    OTs = Ring([sb(f"xattnT{i}", [P, GT], F32, mem) for i in range(2)])
    xr = Ring([sb(f"xrecip{i}", [P, 4, 2], F32, mem) for i in range(2)])
    xst_lanes = [q.lane(f"xq_stack{i}_loaded") for i in range(3)]
    xg_lanes = [q.lane(f"x_group{j}_loaded") for j in range(XPAIRS)]
    x2_lanes = [q.lane(f"x2_stored{j}") for j in range(XPAIRS)]

    def split_weight(hi, lo, raw, waits, on_scalar=False):
        if on_scalar:
            th = act(lambda e: e.activation(hi, raw, ACT.Copy), waits)
        else:
            th = pool(lambda e: e.tensor_scalar(hi, raw, 1.0, 0.0, ALU.mult, ALU.add), waits)
        tl = dve(lambda e: e.tensor_tensor(lo, raw, hi.bitcast(F32), ALU.subtract), [th])
        return [th, tl]

    raw_lanes = [q.lane(f"raw_weights{i}_loaded") for i in range(4)]
    raw_qd = xg[:, 0, :].rearrange("p (k n) -> p k n", k=KB)
    raw_kvd = xg[:, 1, 0:KB * XD].rearrange("p (k n) -> p k n", k=KB)
    raw_ok = {}

    def load_raw_weights():
        raw_ok["qd"] = q.dma(raw_lanes[0], raw_qd, wq_d.rearrange("(k p) n -> p k n", p=P))
        raw_ok["kvd"] = q.dma(raw_lanes[1], raw_kvd, wkv_d.rearrange("(k p) n -> p k n", p=P))
        raw_ok["qk"] = q.dma(raw_lanes[2], xg[:, 2, :], w_qk)
        q.dma(raw_lanes[3], xg[0:XD, 3, :], wv_u)
        raw_ok["vu"] = q.dma(raw_lanes[3], xg[XD:P, 3, :], wv_u)

    wqd_ok, wkv_ok, wqk_ok, wvu_ok = [], [], [], []

    def split_wqd():
        wqd_ok.extend(split_weight(wqd[0][:, :, :], wqd[1][:, :, :], raw_qd, [raw_ok["qd"]]))

    def split_wkv():
        for c in range(2):
            wkv_ok.extend(split_weight(wkv[0][:, :, c, :], wkv[1][:, :, c, :], raw_kvd, [raw_ok["kvd"]]))

    def split_wqk():
        wqk_ok.extend(split_weight(wqk[0][:, :], wqk[1][:, :], xg[:, 2, :], [raw_ok["qk"]]))

    def split_wvu():
        t = pool(lambda e: e.tensor_scalar(wvu[:, :], xg[:, 3, :], 1.0, 0.0, ALU.mult, ALU.add), [raw_ok["vu"]])
        wvu_ok.append(dve(lambda e: e.tensor_tensor(wvu[XD:P, :], xg[XD:P, 3, :], wvu[XD:P, :].bitcast(F32),
                                                    ALU.subtract), [t]))

    def split_bank(J, jk, t, hi, lo, waits, scale=None):
        if scale is None:
            th = act(lambda e: e.activation(hi, J[:, :], ACT.Copy), [t] + waits)
            tl = dve(lambda e: e.tensor_tensor(lo, J[:, :], hi.bitcast(F32), ALU.subtract), [th] + waits)
        else:
            th = act(lambda e: e.activation(hi, J[:, :], ACT.Copy, scale=scale), [t] + waits)
            tl = dve(lambda e: e.scalar_tensor_tensor(lo, J[:, :], scale, hi.bitcast(F32), ALU.mult, ALU.subtract),
                     [th] + waits)
        proj.used(jk, tl)
        return [th, tl]

    def down_three(J, users, w, parts, ready):
        n = 0
        for kb in range(KB):
            for wp, ap in PASSES:
                last = kb == KB - 1 and wp == 1
                t = pe(lambda e, kb=kb, wk=w(wp, kb), ap=ap, first=n == 0, last=last: e.matmul(
                    J[:, :], wk, parts[ap][:, kb, :], start=first, stop=last), ready + users, last)
                n += 1
        return t

    def turned_group(g, src, waits, normed):
        state, loads, norms, turns = {"ready": []}, [], [], []
        for m in range(TILES):
            def load(m=m):
                state[m] = load_rows(rows(src, g * TILES + m), waits)

            def norm(m=m):
                if normed:
                    buf, read, loaded = state[m]
                    state[m] = buf, read, layernorm(buf, loaded)

            def turn(half, m=m):
                if m == 0 and half == 0:
                    state["parts"], state["users"], state["k"] = actT.take()
                if half == 0:
                    buf, read, ok = state[m]
                    state["p"] = transpose_tile(buf, ok, state["parts"][0], state["parts"][1], m, state["users"], read)
                r = state["p"][half]()
                return lambda: state["ready"].extend(r())
            loads.append(load)
            norms.append(norm)
            turns += [lambda turn=turn, half=half: turn(half) for half in range(2)]
        return state, loads, norms, turns

    cq_users, xv_users = [], []
    x2_stored = []
    cols = lambda a, g, j: a[g * GT:(g + 1) * GT, j * P:(j + 1) * P].rearrange("(a p) n -> p a n", p=P)
    xg_loaded, xg_reload = {}, []

    def cross_unit(g, j, kv, kvk, kv_ok, v_ok, stacks, n_heads=2 * GB):
        box = {}
        st, sk, ready = stacks[j]

        def begin():
            box["sums"], box["su"], box["sk"] = row_sums.take()

        def mk_scores(i, S, waits):
            b, r = divmod(i, 2)
            for a in range(QT):
                for part in range(2):
                    t = pe(lambda e, a=a, part=part: e.matmul(
                        S[:, a * SEQ:(a + 1) * SEQ], st[:, r, b * SEQ + a * P:b * SEQ + (a + 1) * P],
                        kv[:, part, b * SEQ:(b + 1) * SEQ], start=part == 0, stop=part == 1),
                        waits + [ready] + kv_ok + box["su"], a == QT - 1 and part == 1)
            if i == n_heads - 1:
                xst.used(sk, t)
                if j == XPAIRS - 1:
                    ckv.used(kvk, t)
            return t

        def sums(i, a):
            b, r = divmod(i, 2)
            return box["sums"][:, b * QT + a, r:r + 1]

        def values(b, pts):
            if b == 0:
                box["O"], box["ou"], box["ok"] = attn.take()
            O = box["O"]
            for kt in range(QT):
                for r in range(2):
                    PT, ptk, tp = pts[r]
                    t = pe(lambda e, kt=kt, r=r, PT=PT: e.matmul(
                        O[r * XD:(r + 1) * XD, b * SEQ:(b + 1) * SEQ],
                        xv[:, b * QT + kt, (2 * j + r) * XD:(2 * j + r + 1) * XD],
                        PT[:, kt * SEQ:(kt + 1) * SEQ], start=kt == 0, stop=kt == QT - 1,
                        tile_position=(0, r * XD)), [tp] + v_ok + box["ou"], kt == QT - 1)
                    if kt == QT - 1:
                        probT.used(ptk, t)
            box["o_t"] = t
            if j == XPAIRS - 1:
                xv_users[:] = [t]

        def end():
            rc, ru, rk = xr.take()
            tr = dve(lambda e: e.reciprocal(rc[:, :, :], box["sums"][:, :, 0:2]), [box["exp"]] + ru)
            row_sums.used(box["sk"], tr)
            return [lambda: copy(), lambda: finish(tr, rc, rk)]

        def copy():
            o, ou, ok = OTs.take()
            box["copied"] = act(lambda e: e.activation(o[:, :], box["O"][:, :], ACT.Copy), [box["o_t"]] + ou)
            attn.used(box["ok"], box["copied"])
            box["copy"] = o, ok

        def finish(tr, rc, rk):
            o, ok = box["copy"]
            t = box["copied"]
            J, users, jk = proj.take()
            for a in range(TILES):
                t2 = pe(lambda e, a=a: e.transpose(J[:, a * P:(a + 1) * P], o[:, a * P:(a + 1) * P], ident[:, :]),
                        [t] + users, a == TILES - 1)
            OTs.used(ok, t2)
            y, yu, yk = tmp.take()
            heads4 = lambda a: a.rearrange("p (a r d) -> p a r d", a=TILES, r=2)
            t3 = dve(lambda e: e.tensor_tensor(
                heads4(y[:, :]), heads4(J[:, :]),
                rc[:, :, :].rearrange("p a (r o) -> p a r o", o=1).to_broadcast([P, TILES, 2, XD]), ALU.mult),
                [t2, tr] + yu)
            proj.used(jk, t3)
            xr.used(rk, t3)
            xs = xg[:, :, j * P:(j + 1) * P]
            t4 = pool(lambda e: e.tensor_tensor(xs, xs, y[:, :].rearrange("p (a n) -> p a n", a=TILES), ALU.add),
                      [t3, xg_loaded[j]])
            tmp.used(yk, t4)
            stored = q.dma(x2_lanes[j], cols(x2, g, j), xs, [t4])
            x2_stored.append(stored)
            for again in xg_reload:
                again()
            xg_reload.clear()
            if g + 1 < NG:
                def again():
                    xg_loaded[j] = q.dma(xg_lanes[j], xs, cols(x1, g + 1, j), [stored])
                xg_reload.append(again)
        return dict(heads=n_heads, set=2, box=box, begin=begin, scores=mk_scores, sums=sums,
                    values=values, end=end)

    def low_rank(state, w, waits):
        J, users, jk = proj.take()
        t = down_three(J, users, w, state["parts"], state["ready"] + waits)
        actT.used(state["k"], t)
        return lambda hi, lo, hl_users: split_bank(J, jk, t, hi, lo, hl_users)

    def v_up(kv, kv_ok, m, n):
        J, users, jk = proj.take()
        for part in range(2):
            t = pe(lambda e, part=part: e.matmul(
                J[:, :], kv[:, part, m * P:(m + 1) * P], wvu[:, n * GT:(n + 1) * GT],
                start=part == 0, stop=part == 1), kv_ok + wvu_ok + users, part == 1)
        dst = xv[:, m, n * GT:(n + 1) * GT]
        if n:
            t = act(lambda e: e.activation(dst, J[:, :], ACT.Copy), [t] + xv_users)
        else:
            t = dve(lambda e: e.tensor_copy(dst, J[:, :]), [t] + xv_users)
        proj.used(jk, t)
        return t

    def xq_piece(j, stacks, cq_ok):
        def mm():
            J, users, jk = proj.take()
            for n, (wp, ap) in enumerate(PASSES):
                t = pe(lambda e, wp=wp, ap=ap, n=n: e.matmul(
                    J[:, :], wqk[wp][:, j * P:(j + 1) * P], cq[:, ap, :], start=n == 0, stop=n == 2),
                    cq_ok + wqk_ok + users, n == 2)
            if j == XPAIRS - 1:
                cq_users[:] = [t]

            def rest():
                b, bu, bk = hl.take()
                th, tl = split_bank(J, jk, t, b[:, 0, :], b[:, 1, :], bu, XD ** -0.5)
                st, su, sk = xst.take()
                for part, tok in ((0, th), (1, tl)):
                    for r in range(2):
                        t2 = q.dma(xst_lanes[sk], st[part * XD:(part + 1) * XD, r, :].bitcast(F32),
                                   b[r * XD:(r + 1) * XD, part, :].bitcast(F32), [tok] + su)
                hl.used(bk, t2)
                stacks[j] = (st, sk, t2)
            return rest
        return mm

    def group_inputs(g):
        xs, *x_work = turned_group(g, x1, list(x1_stored.values()), True)
        cs, *c_work = turned_group(g, ctx_in, [], False)
        return xs, cs, *[a + b for a, b in zip(x_work, c_work)]

    xs, cs, loads, norms, turns = group_inputs(0)
    for m in range(3):
        xs[m] = cross_first[m]
    for i, tile in enumerate((0, 1, 2, 4, 5, 3, 6, 7)):
        run(turns[2 * tile])
        run(turns[2 * tile + 1])
        if i < 5:
            loads[i + 3]()
        if i == 2:
            load_raw_weights()
            norms[3]()
        if i >= 4:
            (split_wqd, split_wkv, split_wqk, split_wvu)[i - 4]()
        if i == 6:
            cq_ok = low_rank(xs, lambda wp, kb: wqd[wp][:, kb, :], wqd_ok)(cq[:, 0, :], cq[:, 1, :], cq_users)
    for j in range(XPAIRS):
        xg_loaded[j] = q.dma(xg_lanes[j], xg[:, :, j * P:(j + 1) * P], cols(x1, 0, j),
                             wqd_ok + wkv_ok + wqk_ok + wvu_ok + list(x1_stored.values()))
    late, ffn_first = [], []
    for g in range(NG):
        if g:
            cq_ok = low_rank(xs, lambda wp, kb: wqd[wp][:, kb, :], wqd_ok)(cq[:, 0, :], cq[:, 1, :], cq_users)
        for f in late:
            f()
        stacks = {}
        run(xq_piece(0, stacks, cq_ok))
        run(xq_piece(1, stacks, cq_ok))
        ckv_split = low_rank(cs, lambda wp, kb: wkv[wp][:, kb, :, :].rearrange("p c n -> p (c n)"), wkv_ok)
        kv, ku, kvk = ckv.take()
        kv_ok = ckv_split(kv[:, 0, :], kv[:, 1, :], ku)
        if g == 0:
            nxt = group_inputs(1)
            for i in range(3):
                nxt[2][i]()
        v_ok = []
        v_pieces = [lambda m=m, n=n: v_ok.append(v_up(kv, kv_ok, m, n)) for m in range(TILES) for n in range(2)]
        for piece in v_pieces[:5]:
            piece()

        plan = {}
        for j in range(XPAIRS):
            if j + 2 < XPAIRS:
                plan[j, 1] = [xq_piece(j + 2, stacks, cq_ok)]
            if g + 1 < NG:
                xs, cs, loads, norms, turns = nxt
                plan[j, 0] = [turns[2 * j]]
                plan[j, 0] += [norms[j + 1]] if j + 1 < len(norms) else []
                plan[j, 3] = [turns[2 * j + 1]] + ([loads[j + 3]] if j + 3 < len(loads) else [])
        lead = v_pieces[5:]
        if g + 1 < NG:
            lead.insert(0, nxt[3][0])
        if g + 2 < NG:
            nxt = group_inputs(g + 2)
            for j in range(3):
                plan[5 + j, 3].append(nxt[2][j])
        units = [{"heads": 2 * GB, "on_scalar": ON_SCALAR_CROSS,
                  "make": lambda j=j: cross_unit(g, j, kv, kvk, kv_ok, v_ok, stacks)}
                 for j in range(XPAIRS)]
        if g + 1 == NG:
            stored = x2_stored[0:XPAIRS]
            for j in range(TILES):
                def ffn_load(j=j):
                    ffn_first.append(load_rows(rows(x2, j), stored, tiles_in if j < 3 else residuals))

                def ffn_norm(j=j):
                    buf, read, loaded = ffn_first[j]
                    ffn_first[j] = buf, read, layernorm(buf, loaded)
                plan.setdefault((3 + j, 0), []).append(ffn_load)
                plan.setdefault((4 + j, 0), []).append(ffn_norm)
        late = attention(units, lambda n: plan.get(divmod(n, 2 * GB), []), lead)
    for f in late:
        f()
    q.phase_end()
    mem.close()
    attn_mem.close()

    mem = ExitStack()
    actT = Ring([[sb(f"hT3_{n}", [P, KB, GT], F32R, mem) for n in ("hi", "lo")]])
    u1s = [sb(f"u1_{n}", [P, KB, RANK], F32R, mem) for n in ("hi", "lo")]
    v2s = [sb(f"v2_{n}", [P, RB, D], F32R, mem) for n in ("hi", "lo")]
    v1_all = sb("v1_all", [P, RB, 2, INTER], F32, mem)
    u2_all = sb("u2_all", [P, FB, RANK], F32, mem)
    v1s = Ring([[sb(f"v1_{n}{i}", [P, 2, RB, P], F32R, mem) for n in ("hi", "lo")] for i in range(3)])
    u2s = Ring([[sb(f"u2_{n}{i}", [P, RB, P], F32R, mem) for n in ("hi", "lo")] for i in range(3)])
    pT = Ring([[sb(f"pT{i}_{n}", [P, RB, GT], F32R, mem) for n in ("hi", "lo")] for i in range(2)])
    inner = Ring([sb(f"inner{i}", [P, GT], F32, mem) for i in range(2)])
    inner_hl = Ring([sb(f"inner_hl{i}", [P, 2, GT], F32R, mem) for i in range(2)])
    zT = [sb(f"zT_{n}", [P, RB, GT], F32R, mem) for n in ("hi", "lo")]
    b1c = sb("b1_cols", [P, 2 * FB], F32, mem)
    b2_all = sb("b2_all", [P, D], F32, mem)
    b1_lane, b2_lane = q.lane("b1_loaded"), q.lane("b2_loaded")
    CB = 4
    w_lanes = [q.lane(f"inner_weights{i}_loaded") for i in range((FB + CB - 1) // CB)]

    def in_group(g):
        state, loads, norms, turns = turned_group(g, x2, x2_stored[g * XPAIRS:(g + 1) * XPAIRS], True)
        box = {"state": state}

        def down(r, c, n_chunks):
            if c == 0:
                box["J"] = proj.take()
                if r == 0:
                    box["p"], box["pu"], box["pk"] = pT.take()
                    box["ok"] = []
            J, users, jk = box["J"]
            for kb in range(c * KB // n_chunks, (c + 1) * KB // n_chunks):
                for n, (wp, ap) in enumerate(PASSES):
                    last = kb == KB - 1 and n == 2
                    t = pe(lambda e, kb=kb, wp=wp, ap=ap, first=kb == 0 and n == 0, last=last: e.matmul(
                        J[:, :], u1s[wp][:, kb, r * P:(r + 1) * P], state["parts"][ap][:, kb, :], start=first,
                        stop=last), state["ready"] + u1_ok + users, last)
            if c < n_chunks - 1:
                return None
            if r == RB - 1:
                actT.used(state["k"], t)
            parts = box["p"]
            return lambda: box["ok"].extend(split_bank(J, jk, t, parts[0][:, r, :], parts[1][:, r, :], box["pu"]))
        return box, loads, norms, turns, [lambda r=r, c=c: down(r, c, 2) for r in range(RB) for c in range(2)]

    box, loads, norms, turns, downs = in_group(0)
    for m in range(TILES):
        box["state"][m] = ffn_first[m]
    u1_ok, v2_ok = [], []
    u1_raw = {}

    def load_u1(i, ring, lanes):
        buf, users, k = ring.take()
        b3 = buf[:, :].rearrange("p (k n) -> p k n", k=4)
        t = q.dma(lanes[k], b3, u1[i * 4 * P:(i + 1) * 4 * P, :].rearrange("(k p) n -> p k n", p=P), users)
        u1_raw[i] = b3, ring, k, t

    def split_u1(i):
        b3, ring, k, t = u1_raw[i]
        ok = split_weight(u1s[0][:, 4 * i:4 * i + 4, :], u1s[1][:, 4 * i:4 * i + 4, :], b3, [t])
        ring.used(k, *ok)
        u1_ok.extend(ok)

    load_u1(0, *residuals)

    def load_inner_weights(c):
        c0, c1 = c * CB * P, min(INTER, (c + 1) * CB * P)
        for half in range(2):
            t = q.dma(w_lanes[c], v1_all[:, :, half, c0:c1],
                      v1[:, half * INTER + c0:half * INTER + c1].rearrange("(r p) n -> p r n", p=P))
        f1 = c1 // P
        t = q.dma(w_lanes[c], u2_all[:, c * CB:f1, :], u2[c0:f1 * P, :].rearrange("(f p) n -> p f n", p=P))
        if f1 * P < c1:
            t = q.dma(w_lanes[c], u2_all[0:FLAST, FB - 1, :], u2[f1 * P:c1, :], [u2_zero])
        return t

    u2_zero = pool(lambda e: e.memset(u2_all[:, FB - 1, :], 0.0))
    b1_rows, _, b1_k = inner.take()

    def load_b1():
        t = pool(lambda e: e.memset(b1_rows[0:2 * FB, 0:P], 0.0))
        for i in range(2):
            q.dma(b1_lane, b1_rows[i * FB:i * FB + FB - 1, 0:P],
                  b1[i * INTER:i * INTER + (FB - 1) * P].rearrange("(a b) -> a b", b=P), [t])
            t2 = q.dma(b1_lane, b1_rows[i * FB + FB - 1:i * FB + FB, 0:FLAST],
                       b1[i * INTER + (FB - 1) * P:(i + 1) * INTER].rearrange("(a b) -> a b", a=1), [t])
        return t2

    for i in range(2 * TILES):
        run(turns[i])
        if i == 1:
            load_u1(1, *tiles_in)
            w_loaded = {0: load_inner_weights(0)}
        if i == 2:
            b1_rows_ok = load_b1()
        if i == 3:
            w_loaded[1] = load_inner_weights(1)
        if i in (1, 3):
            split_u1((i - 1) // 2)
    J, users, jk = proj.take()
    t = pe(lambda e, J=J: e.transpose(J[:, 0:2 * FB], b1_rows[0:2 * FB, 0:P], ident[0:2 * FB, 0:2 * FB]),
           [b1_rows_ok] + users, True)
    inner.used(b1_k, t)
    b1_ok = dve(lambda e, J=J: e.tensor_copy(b1c[:, :], J[:, 0:2 * FB]), [t])
    proj.used(jk, b1_ok)
    for p in downs:
        run(p)

    b2_ok = q.dma(b2_lane, b2_all[:, :], b2.rearrange("(o n) -> o n", o=1).to_broadcast([P, D]))

    def load_v2(i):
        buf, users, k = xres.take()
        t = q.dma(xres_lanes[k], buf[:, :], rows(v2, i), users)
        ok = split_weight(v2s[0][:, i, :], v2s[1][:, i, :], buf[:, :], [t], on_scalar=True)
        xres.used(k, *ok)
        v2_ok.extend(ok)

    gate_up = Ring(bank[0:4])
    z_banks = [bank[4], bank[5]]

    def inner_weights(f):
        (hi, lo), su, sk = v1s.take()
        ready = [w_loaded[f // CB]] + su
        n = P if f < FB - 1 else FLAST
        if n < P:
            ready = [pool(lambda e, a=a: e.memset(a[:, :, :, :].bitcast(F32), 0.0), su) for a in (hi, lo)] + ready
        gu = v1_all[:, :, :, f * P:f * P + n].rearrange("p r s n -> p s r n")
        th = act(lambda e: e.activation(hi[:, :, :, 0:n], gu, ACT.Copy), ready)
        tl = pool(lambda e: e.tensor_tensor(lo[:, :, :, 0:n], gu, hi[:, :, :, 0:n].bitcast(F32), ALU.subtract), [th])
        return (hi, lo), sk, [th, tl]

    def down_weights(f):
        (zh, zl), zu, zk = u2s.take()
        u2f = u2_all[:, f, :].rearrange("p (r n) -> p r n", r=RB)
        ok = split_weight(zh[:, :, :], zl[:, :, :], u2f, [w_loaded[f // CB]] + zu, on_scalar=True)
        return (zh, zl), zk, ok

    def gate_up_stage(f, w, wk_, w_ok, parts, p_ok):
        banks = []
        for s in range(2):
            G, gu, gk = gate_up.take()
            for r in range(RB):
                for n, (wp, ap) in enumerate(PASSES):
                    last = r == RB - 1 and n == 2
                    t = pe(lambda e, G=G, s=s, r=r, n=n, wp=wp, ap=ap, last=last: e.matmul(
                        G[:, :], w[wp][:, s, r, :], parts[ap][:, r, :],
                        start=r == 0 and n == 0, stop=last), w_ok + p_ok + gu, last)
            banks.append((G, gk, t))
        v1s.used(wk_, t)
        (G, gk, tg), (U, uk, tu) = banks
        a, au, ak = inner.take()
        t = act(lambda e: e.activation(a[:, :], G[:, :], ACT.Silu, bias=b1c[:, f:f + 1]), [tg, b1_ok] + au)
        gate_up.used(gk, t)
        t = dve(lambda e: e.scalar_tensor_tensor(a[:, :], U[:, :], b1c[:, FB + f:FB + f + 1], a[:, :],
                                                 ALU.add, ALU.mult), [t, tu])
        gate_up.used(uk, t)
        b, bu, bk = inner_hl.take()
        th = act(lambda e: e.activation(b[:, 0, :], a[:, :], ACT.Copy), [t] + bu)
        tl = dve(lambda e: e.tensor_tensor(b[:, 1, :], a[:, :], b[:, 0, :].bitcast(F32), ALU.subtract), [th] + bu)
        inner.used(ak, tl)
        return (b, bk, [th, tl]), tu

    z_users, zT_users = [], []
    last_lanes = [q.lane(f"last_out_stored{m}") for m in range(TILES)]

    def z_stage(f, b, bk, b_ok, w, wk_, w_ok):
        for r in range(RB):
            for n, (wp, ap) in enumerate(PASSES):
                t = pe(lambda e, r=r, n=n, wp=wp, ap=ap: e.matmul(
                    z_banks[r][:, :], w[wp][:, r, :], b[:, ap, :], start=f == 0 and n == 0,
                    stop=f == FB - 1 and n == 2, skip_group_check=True), b_ok + w_ok + z_users,
                    r == RB - 1 and n == 2)
        inner_hl.used(bk, t)
        u2s.used(wk_, t)
        return t

    def z_split(t):
        ok = []
        for r in range(RB):
            hi, lo = (a[:, r, :] for a in zT)
            th = act(lambda e, r=r, hi=hi: e.activation(hi, z_banks[r][:, :], ACT.Copy), [t] + zT_users)
            tl = dve(lambda e, r=r, hi=hi, lo=lo: e.tensor_tensor(lo, z_banks[r][:, :], hi.bitcast(F32),
                                                                  ALU.subtract), [th] + zT_users)
            ok += [th, tl]
        z_users[:] = ok
        return ok

    def out_group(g):
        state, loads, pieces = {}, [], []

        def load(m):
            ring, lanes = (xin, xin_lane) if g == NG - 1 and m >= 2 else (xres, xres_lanes)
            buf, users, k = ring.take()
            t = q.dma(lanes[k], buf[:, :], rows(x2, g * TILES + m), users + x2_stored[g * XPAIRS:(g + 1) * XPAIRS])
            state[m] = buf, k, t

        def piece(m, n):
            buf, k, loaded = state[m]
            J, users, jk = proj.take()
            for r in range(RB):
                for i, (wp, ap) in enumerate(PASSES):
                    last = r == RB - 1 and i == 2
                    t = pe(lambda e, r=r, i=i, wp=wp, ap=ap, last=last: e.matmul(
                        J[:, :], zT[ap][:, r, m * P:(m + 1) * P], v2s[wp][:, r, n * GT:(n + 1) * GT],
                        start=r == 0 and i == 0, stop=last), state["z"] + v2_ok + users, last)
            zT_users[:] = [t]

            def rest():
                xs = buf[:, n * GT:(n + 1) * GT]
                t2 = dve(lambda e: e.tensor_tensor(xs, xs, b2_all[:, n * GT:(n + 1) * GT], ALU.add), [loaded, b2_ok])
                t2 = dve(lambda e: e.tensor_tensor(xs, J[:, :], xs, ALU.add), [t, t2])
                proj.used(jk, t2)
                if n == 1:
                    if g == NG - 1:
                        q.dma(last_lanes[m], rows(out, g * TILES + m), buf[:, :], [t2])
                    else:
                        xres.used(k, q.dma(store_lanes[k], rows(out, g * TILES + m), buf[:, :], [t2]))
            return rest
        for m in range(TILES):
            loads.append(lambda m=m: load(m))
            pieces += [lambda m=m, n=n: piece(m, n) for n in range(2)]
        return state, loads, pieces

    weights = {0: inner_weights(0), 1: inner_weights(1)}
    out_state = {}
    out_loads, out_pieces = [], []
    for g in range(NG):
        p_ok, parts, pk = box["ok"], box["p"], box["pk"]
        plan = {f: [] for f in range(FB)}
        for i, piece in enumerate(out_pieces):
            plan[i + 1].append(piece)
            if i in (1, 3):
                plan[i + 2].append(out_loads[i // 2 + 2])
        if g + 1 < NG:
            box, loads, norms, turns, downs = in_group(g + 1)
            for i, f in enumerate((5, 6, 7, 11)):
                plan[f].append(loads[i])
                plan[f + 1].append(norms[i])
            for i, piece in enumerate(turns):
                plan[i + 9].append(piece)
            for i, piece in enumerate(downs):
                plan[i + 17].append(piece)
        out_state, out_loads, out_pieces = out_group(g)
        if g == 0:
            for c in range(2, len(w_lanes)):
                def more(c=c):
                    w_loaded[c] = load_inner_weights(c)
                plan[CB * (c - 2)].insert(0, more)
            for i in range(RB):
                plan[3 + CB * i].append(lambda i=i: load_v2(i))
        plan[FB - 2].append(out_loads[0])
        plan[FB - 1].append(out_loads[1])
        if g == NG - 1:
            plan[FB - 1] += out_loads[2:]
        pending = None
        for f in range(FB):
            v, vk, v_ok = weights.pop(f)
            z_weights = down_weights(f)
            if f + 2 < FB or g + 1 < NG:
                weights[(f + 2) % FB] = inner_weights((f + 2) % FB)
            inner_parts, t_gu = gate_up_stage(f, v, vk, v_ok, parts, p_ok)
            rests = [piece() for piece in plan[f]]
            if pending:
                z_stage(*pending)
            pending = (f, *inner_parts, *z_weights)
            for r in rests:
                if r:
                    r()
        pT.used(pk, t_gu)
        out_state["z"] = z_split(z_stage(*pending))
    for piece in out_pieces:
        run(piece)
    q.phase_end()
    ends = list(q.gate["sync"])
    mem.close()

    with nc.Block() as block:
        @block.sync
        def _(eng):
            q.emit("sync", eng)
            for sem, value in ends:
                eng.wait_ge(sem, value)

        @block.tensor
        def _(eng):
            q.emit("tensor", eng)

        @block.scalar
        def _(eng):
            q.emit("scalar", eng)

        @block.vector
        def _(eng):
            q.emit("vector", eng)

        @block.gpsimd
        def _(eng):
            q.emit("gpsimd", eng)
    ctx.close()


_INS = ["x", "ctx_4096", "L0_attn_q_weight", "L0_attn_q_scale", "L0_attn_k_weight", "L0_attn_k_scale",
        "L0_attn_v_weight", "L0_attn_v_scale", "L0_attn_o_weight", "L0_attn_o_scale", "L0_xattn_Wq_d",
        "L0_xattn_W_qk", "L0_xattn_Wkv_d", "L0_xattn_Wv_u", "L0_ffn_U1", "L0_ffn_V1", "L0_ffn_U2", "L0_ffn_V2",
        "L0_ffn_b1", "L0_ffn_b2"]


def kernel(**inputs):
    import concourse.bacc as bacc
    import numpy as np
    from concourse.bass_utils import run_bass_kernel_spmd

    nc = bacc.Bacc("TRN2", target_bir_lowering=False, num_devices=1)
    arrays, args = {}, []
    for name in _INS:
        a = np.ascontiguousarray(inputs[name])
        if name in ("x", "ctx_4096"):
            a = a.reshape(TOK, D)
        arrays[f"in_{name}"] = a
        args.append(nc.dram_tensor(f"in_{name}", a.shape, mybir.dt.from_np(a.dtype), kind="ExternalInput").ap())
    args.append(nc.dram_tensor("out", (TOK, D), F32, kind="ExternalOutput").ap())
    build_program(nc, *args)
    r = run_bass_kernel_spmd(nc, [arrays], core_ids=[0])
    return r.results[0]["out"].reshape(BATCH, SEQ, D)
```
